# Optimizing a Trainium2 kernel written in Bass

```python
import numpy as np
import jax
import jax.numpy as jnp

def _softmax(x, axis=-1):
    return jax.nn.softmax(x, axis=axis)

def _gelu(x):
    return jax.nn.gelu(x, approximate=True)

def _silu(x):
    return jax.nn.silu(x)

def _sigmoid(x):
    return jax.nn.sigmoid(x)

def _layernorm(x, axis=-1, eps=1e-05):
    m = jnp.mean(x, axis=axis, keepdims=True)
    v = jnp.var(x, axis=axis, keepdims=True)
    return (x - m) / jnp.sqrt(v + eps)

def _scatter_add(tgt, idx, src, axis=0):
    return tgt.at[idx].add(src)

def _segment_sum(src, seg, n):
    return jax.ops.segment_sum(src, seg, n)
kernel_name = 'mk_recurrent_d1_jaxref_r8_423945'

def setup_inputs(seed: int=0):
    np.random.seed(seed)
    _w = jnp.asarray

    def _L0_attn_setup():
        import jax, jax.numpy as jnp
        import numpy as np
        D_MODEL = 128
        HEADDIM = 128
        D_STATE = 64
        NGROUPS = 1
        NHEADS = D_MODEL // HEADDIM

        def segsum(x):
            T = x.shape[-1]
            xe = jnp.broadcast_to(x[..., None], x.shape + (T,))
            mask_lower = jnp.tril(jnp.ones((T, T), dtype=bool), k=-1)
            xe = jnp.where(mask_lower, xe, 0.0)
            x_segsum = jnp.cumsum(xe, axis=-2)
            mask_incl = jnp.tril(jnp.ones((T, T), dtype=bool), k=0)
            return jnp.where(mask_incl, x_segsum, -jnp.inf)

        def ssd_minimal_discrete(X, A, B, C, chunk):
            b, T = (X.shape[0], X.shape[1])
            c = T // chunk
            resh = lambda t: t.reshape(b, c, chunk, *t.shape[2:])
            X, B, C = (resh(X), resh(B), resh(C))
            A = resh(A).transpose(0, 3, 1, 2)
            A_cumsum = jnp.cumsum(A, axis=-1)
            Lmat = jnp.exp(segsum(A))
            Y_diag = jnp.einsum('bclhn,bcshn,bhcls,bcshp->bclhp', C, B, Lmat, X)
            decay_states = jnp.exp(A_cumsum[..., -1:] - A_cumsum)
            states = jnp.einsum('bclhn,bhcl,bclhp->bchpn', B, decay_states, X)
            init = jnp.zeros_like(states[:, :1])
            states = jnp.concatenate([init, states], axis=1)
            A_last = jnp.pad(A_cumsum[..., -1], ((0, 0), (0, 0), (1, 0)))
            decay_chunk = jnp.exp(segsum(A_last))
            new_states = jnp.einsum('bhzc,bchpn->bzhpn', decay_chunk, states)
            states = new_states[:, :-1]
            state_decay_out = jnp.exp(A_cumsum)
            Y_off = jnp.einsum('bclhn,bchpn,bhcl->bclhp', C, states, state_decay_out)
            return (Y_diag + Y_off).reshape(b, T, NHEADS, HEADDIM)

        def ssd_forward(x, W_xproj, dt_bias, A_log, D):
            b, T, _ = x.shape
            dtBC = x @ W_xproj.T
            dt = dtBC[..., :NHEADS]
            Bm = dtBC[..., NHEADS:NHEADS + NGROUPS * D_STATE]
            Cm = dtBC[..., NHEADS + NGROUPS * D_STATE:]
            dt = jax.nn.softplus(dt + dt_bias)
            A = -jnp.exp(A_log)
            Xh = x.reshape(b, T, NHEADS, HEADDIM) * dt[..., None]
            Bh = jnp.broadcast_to(Bm.reshape(b, T, NGROUPS, D_STATE), (b, T, NHEADS, D_STATE))
            Ch = jnp.broadcast_to(Cm.reshape(b, T, NGROUPS, D_STATE), (b, T, NHEADS, D_STATE))
            y = ssd_minimal_discrete(Xh, A * dt, Bh, Ch, T)
            y = y.reshape(b, T, D_MODEL)
            D_full = jnp.repeat(D, HEADDIM)
            return y + x * D_full
        key = jax.random.key(seed)
        k1, k2, k3 = jax.random.split(key, 3)
        x = jax.random.normal(k1, (2, 256, D_MODEL), dtype=jnp.float32)
        W_xproj = jax.random.normal(k2, (NHEADS + 2 * NGROUPS * D_STATE, D_MODEL), dtype=jnp.float32) * (1.0 / np.sqrt(D_MODEL))
        dt_bias = jnp.zeros((NHEADS,), dtype=jnp.float32)
        A_log = jnp.log(jax.random.uniform(k3, (NHEADS,), minval=1.0, maxval=16.0, dtype=jnp.float32))
        D = jnp.ones((NHEADS,), dtype=jnp.float32)
        return {'x': x, 'W_xproj': W_xproj, 'dt_bias': dt_bias, 'A_log': A_log, 'D': D}
    _L0_attn_in = _L0_attn_setup()

    def _L0_ffn_setup():
        import jax, jax.numpy as jnp
        import numpy as np
        from jax import lax
        B, S, H = (2, 128, 128)
        I = 64
        E = 32
        TOP_K = 4
        N_GROUP = 4
        TOPK_GROUP = 2
        SCALE = 2.5
        N_SHARED = 2
        SH_I = I * N_SHARED

        def _route(tokens, router_weight, router_bias):
            logits = tokens.astype(jnp.float32) @ router_weight.astype(jnp.float32).T
            scores = jax.nn.sigmoid(logits)
            sfc = scores + router_bias[None, :]
            T = tokens.shape[0]
            grp = sfc.reshape(T, N_GROUP, E // N_GROUP)
            group_scores = lax.top_k(grp, 2)[0].sum(-1)
            _, gidx = lax.top_k(group_scores, TOPK_GROUP)
            gmask = jax.nn.one_hot(gidx, N_GROUP, dtype=sfc.dtype).sum(1)
            smask = jnp.broadcast_to(gmask[:, :, None], (T, N_GROUP, E // N_GROUP)).reshape(T, E)
            tmp = jnp.where(smask > 0, sfc, 0.0)
            _, topk_idx = lax.top_k(tmp, TOP_K)
            topk_w = jnp.take_along_axis(scores, topk_idx, axis=1)
            topk_w = topk_w / (topk_w.sum(-1, keepdims=True) + 1e-20)
            topk_w = topk_w * SCALE
            return (topk_idx, topk_w)
        key = jax.random.key(seed)
        ks = jax.random.split(key, 10)
        std = 0.02
        return {'hidden_states': jax.random.normal(ks[0], (B, S, H), jnp.float32), 'router_weight': jax.random.normal(ks[1], (E, H), jnp.float32) * std, 'router_bias': jnp.zeros((E,), jnp.float32), 'gate_w': jax.random.normal(ks[2], (E, I, H), jnp.float32) * std, 'up_w': jax.random.normal(ks[3], (E, I, H), jnp.float32) * std, 'down_w': jax.random.normal(ks[4], (E, H, I), jnp.float32) * std, 'shared_gate_w': jax.random.normal(ks[5], (SH_I, H), jnp.float32) * std, 'shared_up_w': jax.random.normal(ks[6], (SH_I, H), jnp.float32) * std, 'shared_down_w': jax.random.normal(ks[7], (H, SH_I), jnp.float32) * std}
    _L0_ffn_in = _L0_ffn_setup()
    _d = {'L0_attn_x': _L0_attn_in['x'], 'L0_attn_W_xproj': _L0_attn_in['W_xproj'], 'L0_attn_dt_bias': _L0_attn_in['dt_bias'], 'L0_attn_A_log': _L0_attn_in['A_log'], 'L0_attn_D': _L0_attn_in['D'], 'L0_ffn_router_weight': _L0_ffn_in['router_weight'], 'L0_ffn_router_bias': _L0_ffn_in['router_bias'], 'L0_ffn_gate_w': _L0_ffn_in['gate_w'], 'L0_ffn_up_w': _L0_ffn_in['up_w'], 'L0_ffn_down_w': _L0_ffn_in['down_w'], 'L0_ffn_shared_gate_w': _L0_ffn_in['shared_gate_w'], 'L0_ffn_shared_up_w': _L0_ffn_in['shared_up_w'], 'L0_ffn_shared_down_w': _L0_ffn_in['shared_down_w']}
    _x0 = _d['L0_attn_x']
    _d['L0_attn_x'] = jax.random.normal(jax.random.fold_in(jax.random.key(seed), 1), (8, 512, 128), dtype=_x0.dtype)
    del _x0
    return _d

def reference(L0_attn_x, L0_attn_W_xproj, L0_attn_dt_bias, L0_attn_A_log, L0_attn_D, L0_ffn_router_weight, L0_ffn_router_bias, L0_ffn_gate_w, L0_ffn_up_w, L0_ffn_down_w, L0_ffn_shared_gate_w, L0_ffn_shared_up_w, L0_ffn_shared_down_w):

    def _L0_attn_ref(x, W_xproj, dt_bias, A_log, D):
        import jax, jax.numpy as jnp
        import numpy as np
        D_MODEL = 128
        HEADDIM = 128
        D_STATE = 64
        NGROUPS = 1
        NHEADS = D_MODEL // HEADDIM

        def segsum(x):
            T = x.shape[-1]
            xe = jnp.broadcast_to(x[..., None], x.shape + (T,))
            mask_lower = jnp.tril(jnp.ones((T, T), dtype=bool), k=-1)
            xe = jnp.where(mask_lower, xe, 0.0)
            x_segsum = jnp.cumsum(xe, axis=-2)
            mask_incl = jnp.tril(jnp.ones((T, T), dtype=bool), k=0)
            return jnp.where(mask_incl, x_segsum, -jnp.inf)

        def ssd_minimal_discrete(X, A, B, C, chunk):
            b, T = (X.shape[0], X.shape[1])
            c = T // chunk
            resh = lambda t: t.reshape(b, c, chunk, *t.shape[2:])
            X, B, C = (resh(X), resh(B), resh(C))
            A = resh(A).transpose(0, 3, 1, 2)
            A_cumsum = jnp.cumsum(A, axis=-1)
            Lmat = jnp.exp(segsum(A))
            Y_diag = jnp.einsum('bclhn,bcshn,bhcls,bcshp->bclhp', C, B, Lmat, X)
            decay_states = jnp.exp(A_cumsum[..., -1:] - A_cumsum)
            states = jnp.einsum('bclhn,bhcl,bclhp->bchpn', B, decay_states, X)
            init = jnp.zeros_like(states[:, :1])
            states = jnp.concatenate([init, states], axis=1)
            A_last = jnp.pad(A_cumsum[..., -1], ((0, 0), (0, 0), (1, 0)))
            decay_chunk = jnp.exp(segsum(A_last))
            new_states = jnp.einsum('bhzc,bchpn->bzhpn', decay_chunk, states)
            states = new_states[:, :-1]
            state_decay_out = jnp.exp(A_cumsum)
            Y_off = jnp.einsum('bclhn,bchpn,bhcl->bclhp', C, states, state_decay_out)
            return (Y_diag + Y_off).reshape(b, T, NHEADS, HEADDIM)

        def ssd_forward(x, W_xproj, dt_bias, A_log, D):
            b, T, _ = x.shape
            dtBC = x @ W_xproj.T
            dt = dtBC[..., :NHEADS]
            Bm = dtBC[..., NHEADS:NHEADS + NGROUPS * D_STATE]
            Cm = dtBC[..., NHEADS + NGROUPS * D_STATE:]
            dt = jax.nn.softplus(dt + dt_bias)
            A = -jnp.exp(A_log)
            Xh = x.reshape(b, T, NHEADS, HEADDIM) * dt[..., None]
            Bh = jnp.broadcast_to(Bm.reshape(b, T, NGROUPS, D_STATE), (b, T, NHEADS, D_STATE))
            Ch = jnp.broadcast_to(Cm.reshape(b, T, NGROUPS, D_STATE), (b, T, NHEADS, D_STATE))
            y = ssd_minimal_discrete(Xh, A * dt, Bh, Ch, T)
            y = y.reshape(b, T, D_MODEL)
            D_full = jnp.repeat(D, HEADDIM)
            return y + x * D_full
        return ssd_forward(x, W_xproj, dt_bias, A_log, D)

    def _L0_ffn_ref(hidden_states, router_weight, router_bias, gate_w, up_w, down_w, shared_gate_w, shared_up_w, shared_down_w):
        import jax, jax.numpy as jnp
        import numpy as np
        from jax import lax
        B, S, H = (2, 128, 128)
        I = 64
        E = 32
        TOP_K = 4
        N_GROUP = 4
        TOPK_GROUP = 2
        SCALE = 2.5
        N_SHARED = 2
        SH_I = I * N_SHARED

        def _route(tokens, router_weight, router_bias):
            logits = tokens.astype(jnp.float32) @ router_weight.astype(jnp.float32).T
            scores = jax.nn.sigmoid(logits)
            sfc = scores + router_bias[None, :]
            T = tokens.shape[0]
            grp = sfc.reshape(T, N_GROUP, E // N_GROUP)
            group_scores = lax.top_k(grp, 2)[0].sum(-1)
            _, gidx = lax.top_k(group_scores, TOPK_GROUP)
            gmask = jax.nn.one_hot(gidx, N_GROUP, dtype=sfc.dtype).sum(1)
            smask = jnp.broadcast_to(gmask[:, :, None], (T, N_GROUP, E // N_GROUP)).reshape(T, E)
            tmp = jnp.where(smask > 0, sfc, 0.0)
            _, topk_idx = lax.top_k(tmp, TOP_K)
            topk_w = jnp.take_along_axis(scores, topk_idx, axis=1)
            topk_w = topk_w / (topk_w.sum(-1, keepdims=True) + 1e-20)
            topk_w = topk_w * SCALE
            return (topk_idx, topk_w)
        tokens = hidden_states.reshape(-1, H)
        topk_idx, topk_w = _route(tokens, router_weight, router_bias)
        gate_vals = jax.nn.silu(jnp.einsum('th,eih->tei', tokens, gate_w))
        up_vals = jnp.einsum('th,eih->tei', tokens, up_w)
        hidden_vals = gate_vals * up_vals
        expert_out = jnp.einsum('tei,ehi->teh', hidden_vals, down_w)
        sel = jnp.take_along_axis(expert_out, topk_idx[:, :, None], axis=1)
        mixed = (sel * topk_w[:, :, None].astype(sel.dtype)).sum(1)
        mixed = mixed.reshape(hidden_states.shape)
        sg = jax.nn.silu(jnp.einsum('bsh,ih->bsi', hidden_states, shared_gate_w))
        su = jnp.einsum('bsh,ih->bsi', hidden_states, shared_up_w)
        shared = jnp.einsum('bsi,hi->bsh', sg * su, shared_down_w)
        return mixed + shared
    x = L0_attn_x
    xn = _layernorm(x, axis=-1)
    s = _L0_attn_ref(xn, L0_attn_W_xproj, L0_attn_dt_bias, L0_attn_A_log, L0_attn_D)
    g = _silu(_L0_ffn_ref(xn, L0_ffn_router_weight, L0_ffn_router_bias, L0_ffn_gate_w, L0_ffn_up_w, L0_ffn_down_w, L0_ffn_shared_gate_w, L0_ffn_shared_up_w, L0_ffn_shared_down_w))
    x = x + s * g
    return x

_drawn_inputs = setup_inputs


def setup_inputs(seed=0):
    import zlib

    import numpy as np

    out = dict(_drawn_inputs(seed))
    spreads = {'L0_ffn_router_bias': (0.0, 0.363)}
    factors = {'L0_ffn_router_weight': 3.467,
     'L0_ffn_gate_w': 2.799,
     'L0_ffn_up_w': 2.795,
     'L0_ffn_down_w': 2.758,
     'L0_ffn_shared_gate_w': 2.756,
     'L0_ffn_shared_up_w': 2.726,
     'L0_ffn_shared_down_w': 2.718}
    for name, (base, spread) in spreads.items():
        noise = np.random.default_rng([zlib.crc32(name.encode()), seed]).standard_normal(out[name].shape)
        drawn = base * np.exp(spread * noise) if base else spread * noise
        out[name] = jnp.asarray(drawn.astype(out[name].dtype))
    for name, factor in factors.items():
        out[name] = (out[name] * factor).astype(out[name].dtype)
    return out
```

```python
import concourse.bass as bass
from concourse import mybir
from contextlib import ExitStack

NBLK, T, H = 8, 512, 128
C = 128
NC_ = T // C
E, I = 32, 64
PAIRS = E // 2
U = PAIRS + 1
NS = 64
NG, GE = 4, E // 4
TOPG, TOPK = 2, 4
SCALE = 2.5
LN_EPS = 1e-5
W_EPS = 1e-20
NEG = -30000.0
WT = 98
COL_B, COL_DT = E, E + NS
LAG = 3
HB = 4

K_ID, K_TRI, K_STRICT, K_EYE2, K_BEATS, K_RESET, K_END = 0, 128, 256, 384, 416, 480, 608
P_BIAS, P_DTB, P_ALOG, P_D, P_END = 0, E, E + 1, E + 2, E + 3


def gated_ssd_moe(nc, x_tok, x_feat, w_gate, w_up, w_down, w_small, consts, params, out):
    fp32, f32r, bf16 = mybir.dt.float32, mybir.dt.float32r, mybir.dt.bfloat16
    ALU = mybir.AluOpType
    ACT = mybir.ActivationFunctionType
    AXX = mybir.AxisListType.X
    ctx = ExitStack()
    with ctx:
        def sb(name, shape, dt=fp32):
            return ctx.enter_context(nc.sbuf_tensor(name, shape, dt))

        def sem(name):
            return ctx.enter_context(nc.semaphore(name))

        wg_raw, wu_raw, wd_raw = (sb(n, [128, U * 128]) for n in ("wg_raw", "wu_raw", "wd_raw"))
        wg_hi, wu_hi, wd_hi = (sb(n, [128, U * 128], f32r) for n in ("wg_hi", "wu_hi", "wd_hi"))
        wg_lo, wu_lo, wd_lo = (sb(n, [128, U * 128], f32r) for n in ("wg_lo", "wu_lo", "wd_lo"))
        ws_raw = sb("ws_raw", [128, WT + 128])
        ws_hi = sb("ws_hi", [128, WT + 128], f32r)
        ws_lo = sb("ws_lo", [128, WT + 128], f32r)
        cst = sb("cst", [128, K_END])
        par_sb = sb("par_sb", [128, P_END])
        ones_r = sb("ones_r", [128, 128])
        halfpow = sb("halfpow", [128, NC_])
        eps = sb("eps", [128, NC_])
        sel = sb("sel", [64, E * I], f32r)
        ident_b = sb("ident_b", [128, 128], bf16)
        negm_b = sb("negm_b", [128, NC_ * 128], bf16)
        d_ident = sb("d_ident", [128, 128])
        neg_a = sb("neg_a", [128, 1])
        exp_a = sb("exp_a", [128, 1])
        ident = cst[:, K_ID:K_ID + 128]
        tri = cst[:, K_TRI:K_TRI + 128]
        strict = cst[:, K_STRICT:K_STRICT + 128]
        beats_lm = cst[:, K_BEATS:K_BEATS + NC_ * NG * NG]
        reset = cst[:, K_RESET:K_RESET + NC_ * E]

        xin = [sb(f"xin{k}", [128, NC_, H]) for k in range(2)]
        xf = [sb(f"xf{k}", [128, T]) for k in range(2)]
        xT_hi = [sb(f"xT_hi{k}", [128, T], f32r) for k in range(2)]
        xT_lo = [sb(f"xT_lo{k}", [128, T], f32r) for k in range(2)]
        wT = [sb(f"wT{k}", [64, T], f32r) for k in range(2)]
        yT = [sb(f"yT{k}", [128, T]) for k in range(2)]
        oT = [sb(f"oT{k}", [128, T]) for k in range(2)]
        stats = sb("stats", [128, NC_, 6])
        mv = sb("mv", [128, NC_, 2])
        var_eps = sb("var_eps", [128, NC_])
        rstd = sb("rstd", [128, NC_])
        xn = sb("xn", [128, NC_, H])
        zt = sb("zt", [128, NC_])
        nabs = sb("nabs", [128, NC_])
        sp_e = sb("sp_e", [128, NC_])
        sp_l = sb("sp_l", [128, NC_])
        dt_s = sb("dt_s", [128, NC_])
        dA = sb("dA", [128, NC_])
        mk = sb("mk", [128, NC_, 128])
        Lt = sb("Lt", [128, NC_, 128])
        dec = sb("dec", [128, 8])
        ecum = sb("ecum", [64, 3 * 128])
        dsdt = sb("dsdt", [128, NC_])
        B_tok = sb("B_tok", [128, NC_, NS])
        Bs = sb("Bs", [128, 3, NS])
        BT = sb("BT", [64, T])
        CT = sb("CT", [64, T])
        CTs = sb("CTs", [64, 3 * 128])
        G0 = sb("G0", [128, NC_, 128])
        G = sb("G", [128, NC_, 128])
        St = [sb(f"St{k}", [64, H]) for k in range(3)]
        e_r = sb("e_r", [128, NC_, E])
        r_p1 = sb("r_p1", [128, NC_, E])
        score = sb("score", [128, NC_, E])
        sfc = sb("sfc", [128, NC_ * NG, GE])
        g4h, g4l = sb("g4h", [128, 16, 4]), sb("g4l", [128, 16, 4])
        g2h, g2m, g2x, g2l = (sb(f"g2{n}", [128, 16, 2]) for n in "hmxl")
        g1h, g1m, g1x, g1l = (sb(f"g1{n}", [128, 16, 1]) for n in "hmxl")
        gsum = sb("gsum", [128, NC_, NG])
        gt_ij, ge_ij, gw_ij, bt_ij = (sb(f"{n}_ij", [128, NC_ * NG, NG]) for n in ("gt", "ge", "gw", "bt"))
        grank = sb("grank", [128, NC_ * NG])
        gkeep = sb("gkeep", [128, NC_ * NG])
        cand = sb("cand", [128, NC_ * NG, GE])
        top8 = sb("top8", [128, NC_, 8])
        above = sb("above", [128, NC_, E])
        equal = sb("equal", [128, NC_, E])
        n_above = sb("n_above", [128, NC_])
        room = sb("room", [128, NC_])
        nth = sb("nth", [128, NC_ * E])
        fits = sb("fits", [128, NC_, E])
        tied = sb("tied", [128, NC_, E])
        chosen = sb("chosen", [128, NC_, E])
        w0 = sb("w0", [128, NC_, E])
        wsum = sb("wsum", [128, NC_])
        wsum_e = sb("wsum_e", [128, NC_])
        wrec = sb("wrec", [128, NC_])
        wfull = sb("wfull", [128, NC_, E])
        w_r = sb("w_r", [128, NC_, E], f32r)
        whl = sb("whl", [128, NC_, 2 * E])
        sg = [sb(f"sg{k}", [128, T]) for k in range(2)]
        tt = [sb(f"tt{k}", [128, T]) for k in range(2)]
        hid = [sb(f"hid{k}", [128, T]) for k in range(2)]
        h_hi = [sb(f"h_hi{k}", [128, T], f32r) for k in range(HB + 1)]
        h_lo = [sb(f"h_lo{k}", [128, T], f32r) for k in range(HB + 1)]
        gate_o = sb("gate_o", [128, T])
        yg = sb("yg", [128, T])

        def bank(name):
            return ctx.enter_context(nc.psum_tensor(name, [128, T], fp32))
        G_ps = [bank("G0_ps"), bank("G1_ps")]
        U_ps = [bank("U0_ps"), bank("U1_ps")]
        W_ps, O_ps, SA, SB = bank("W_ps"), bank("O_ps"), bank("SA"), bank("SB")
        SBc = SB[:, :].rearrange("p (t c) -> p t c", t=NC_)
        SAc = SA[:, :].rearrange("p (t c) -> p t c", t=NC_)

        s_cst = sem("s_cst")
        s_wsm = sem("s_wsm")
        s_w = [sem(f"s_w{c}") for c in range(4)]
        s_xin = [sem(f"s_xin{k}") for k in range(2)]
        s_xf = [sem(f"s_xf{k}") for k in range(2)]
        s_setup_p = sem("s_setup_p")
        s_setup_a = sem("s_setup_a")
        s_setup_d = sem("s_setup_d")
        s_wshi = sem("s_wshi")
        s_wslo = sem("s_wslo")
        s_whi = sem("s_whi")
        s_wlo = sem("s_wlo")
        s_dve = sem("s_dve")
        s_pool = sem("s_pool")
        s_stats = sem("s_stats")
        s_rstd = sem("s_rstd")
        s_xn = sem("s_xn")
        s_xnT_ps = sem("s_xnT_ps")
        s_xThi = sem("s_xThi")
        s_xTlo = sem("s_xTlo")
        s_ptok = sem("s_ptok")
        s_pbc = sem("s_pbc")
        s_nabs = sem("s_nabs")
        s_spe = sem("s_spe")
        s_spl = sem("s_spl")
        s_er = sem("s_er")
        s_btok = sem("s_btok")
        s_bt = sem("s_bt")
        s_ct = sem("s_ct")
        s_dt = sem("s_dt")
        s_dA = sem("s_dA")
        s_mk = sem("s_mk")
        s_dec_ps = sem("s_dec_ps")
        s_seg_ps = sem("s_seg_ps")
        s_L = sem("s_L")
        s_dec = sem("s_dec")
        s_ecum = sem("s_ecum")
        s_Bs = sem("s_Bs")
        s_CTs = sem("s_CTs")
        s_sc_ps = sem("s_sc_ps")
        s_st_ps = sem("s_st_ps")
        s_G0 = sem("s_G0")
        s_G = sem("s_G")
        s_S = sem("s_S")
        s_y_ps = sem("s_y_ps")
        s_yT = sem("s_yT")
        s_w_tok = sem("s_w_tok")
        s_wT_ps = sem("s_wT_ps")
        s_wT = sem("s_wT")
        s_gate = sem("s_gate")
        s_up = sem("s_up")
        s_wb = sem("s_wb")
        s_silu = sem("s_silu")
        s_t = sem("s_t")
        s_h = sem("s_h")
        s_hi = sem("s_hi")
        s_lo = sem("s_lo")
        s_down = sem("s_down")
        s_go = sem("s_go")
        s_yg = sem("s_yg")
        s_fin = sem("s_fin")
        s_held = sem("s_held")
        s_out = [sem(f"s_out{k}") for k in range(2)]

        def ready(eng, semaphore, value):
            if isinstance(value, int) and value <= 0:
                return
            eng.wait_ge(semaphore, value)

        def hold(eng, semaphore, value):
            eng.wait_ge(semaphore, value)
            eng.sem_inc(s_held, 1)

        def bc(ap, shape):
            return ap.to_broadcast(shape)

        def slot(i):
            return i % HB if i < PAIRS else HB

        def quarter(c):
            return c * 4 * 128, (c + 1) * 4 * 128 if c < 3 else U * 128

        block = ctx.enter_context(nc.Block())

        @block.sync
        def _(sp):
            sp.dma_start(xin[0][:, :, :], x_tok[0]).then_inc(s_xin[0], 16)
            sp.dma_start(cst[:, :], consts[:, :]).then_inc(s_cst, 16)
            sp.dma_start(par_sb[:, :], params[:, :]).then_inc(s_cst, 16)
            sp.dma_start(ws_raw[:, :], w_small[:, :]).then_inc(s_wsm, 16)
            for c in range(4):
                a, z = quarter(c)
                for dst, src in ((wg_raw, w_gate), (wu_raw, w_up), (wd_raw, w_down)):
                    sp.dma_start(dst[:, a:z], src[:, a:z]).then_inc(s_w[c], 16)
                if c == 1:
                    sp.dma_start(xin[1][:, :, :], x_tok[1]).then_inc(s_xin[1], 16)
            for k in range(2):
                sp.dma_start(xf[k][:, :], x_feat[k]).then_inc(s_xf[k], 16)
            for b in range(NBLK):
                if b + 2 < NBLK:
                    ready(sp, s_xn, NC_ * (b + 1))
                    sp.dma_start(xin[b % 2][:, :, :], x_tok[b + 2]).then_inc(s_xin[b % 2], 16)
                ready(sp, s_fin, b + 1)
                sp.dma_start(out[b], oT[b % 2][:, :]).then_inc(s_out[b % 2], 16)
                if b + 2 < NBLK:
                    sp.wait_ge(s_out[b % 2], 16 * (b // 2 + 1))
                    sp.dma_start(xf[b % 2][:, :], x_feat[b + 2]).then_inc(s_xf[b % 2], 16)
            for k in range(2):
                sp.wait_ge(s_out[k], 16 * NBLK // 2)

        @block.tensor
        def _(pe):
            def three(ps, a_hi, a_lo, x_hi, x_lo):
                nc.tensor.matmul(ps, a_lo, x_hi, start=True, stop=False)
                nc.tensor.matmul(ps, a_hi, x_lo, start=False, stop=False)
                return nc.tensor.matmul(ps, a_hi, x_hi, start=False, stop=True)

            def transpose_xn(n, p):
                ready(pe, s_xn, NC_ * (n + 1))
                ready(pe, s_yT, n)
                for t in range(NC_):
                    m = nc.tensor.transpose(SAc[:, t, :], xn[:, t, :], ident)
                m.then_inc(s_xnT_ps, 1)

            def project(n, p):
                ready(pe, s_xTlo, n + 1)
                ready(pe, s_wT, n)
                for t in range(NC_):
                    c = slice(t * C, (t + 1) * C)
                    m = three(SBc[:, t, 0:WT], xT_hi[p][:, c], xT_lo[p][:, c],
                              ws_hi[:, 0:WT], ws_lo[:, 0:WT])
                m.then_inc(s_ptok, 1)
                three(SA[:, :], ws_hi[:, WT:WT + 128], ws_lo[:, WT:WT + 128],
                      xT_hi[p][:, :], xT_lo[p][:, :]).then_inc(s_pbc, 1)

            def decays(n, p):
                ready(pe, s_er, n + 1)
                ready(pe, s_btok, n + 1)
                ready(pe, s_dA, n + 1)
                nc.tensor.matmul(SB[:, 0:NC_], strict, dA[:, :], start=True, stop=True)
                nc.tensor.matmul(SB[:, NC_:2 * NC_], ones_r[:, :], dA[:, :], start=True, stop=True)
                for t in range(1, NC_):
                    m = nc.tensor.matmul(SB[0:NS, t * C:(t + 1) * C], bc(dA[:, t:t + 1], [128, NS]), tri,
                                         start=True, stop=True)
                m.then_inc(s_dec_ps, 1)
                ready(pe, s_bt, n + 1)
                ready(pe, s_ct, n + 1)
                ready(pe, s_mk, n + 1)
                nc.tensor.matmul(SA[:, :], ident_b[:, :], negm_b[:, :], start=True, stop=False)
                for t in range(NC_):
                    m = nc.tensor.matmul(SAc[:, t, :], mk[:, t, :], tri, start=False, stop=t == NC_ - 1)
                m.then_inc(s_seg_ps, 1)

            def scores(n, p):
                ready(pe, s_L, n + 1)
                for t in range(NC_):
                    c = slice(t * C, (t + 1) * C)
                    m = nc.tensor.matmul(SAc[:, t, :], BT[:, c], CT[:, c], start=True, stop=True)
                m.then_inc(s_sc_ps, 1)
                ready(pe, s_ecum, n + 1)
                ready(pe, s_dec, n + 1)
                ready(pe, s_Bs, n + 1)
                for t in range(NC_ - 1):
                    m = nc.tensor.matmul(SB[0:NS, t * C:(t + 1) * C], Bs[:, t, :], xn[:, t, :],
                                         start=True, stop=True)
                m.then_inc(s_st_ps, 1)

            def mix(n, p):
                ready(pe, s_G, n + 1)
                ready(pe, s_S, n + 1)
                ready(pe, s_CTs, n + 1)
                for t in range(NC_):
                    m = nc.tensor.matmul(SAc[:, t, :], xn[:, t, :], G[:, t, :], start=True, stop=t == 0)
                    if t > 0:
                        m = nc.tensor.matmul(SAc[:, t, :], St[t - 1][:, :], CTs[:, (t - 1) * C:t * C],
                                             start=False, stop=True)
                m.then_inc(s_y_ps, 1)

            def transpose_w(n, p):
                ready(pe, s_w_tok, n + 1)
                hold(pe, s_S, n + 1)
                for t in range(NC_):
                    m = nc.tensor.transpose(SB[0:2 * E, t * C:(t + 1) * C], whl[:, t, :], ident)
                m.then_inc(s_wT_ps, 1)

            side = {3: transpose_xn, 6: project, 10: decays, 12: scores, 14: mix, 15: transpose_w}

            def down(b, i):
                g = U * b + i
                if i == 0:
                    ready(pe, s_go, b)
                ready(pe, s_lo, g + 1)
                c = slice(i * 128, (i + 1) * 128)
                s = slot(i)
                nc.tensor.matmul(O_ps[:, :], wd_lo[:, c], h_hi[s][:, :], start=i == 0, stop=False)
                nc.tensor.matmul(O_ps[:, :], wd_hi[:, c], h_lo[s][:, :], start=False, stop=False)
                nc.tensor.matmul(O_ps[:, :], wd_hi[:, c], h_hi[s][:, :], start=False,
                                 stop=i == U - 1).then_inc(s_down, 1)

            def period(b, p, first=False, last=False):
                for i in range(U):
                    g = U * b + i
                    k = (p + i) % 2
                    c = slice(i * 128, (i + 1) * 128)
                    if first and (i % 4 == 0 and i < PAIRS):
                        pe.wait_ge(s_wlo, 3 * (i // 4 + 1))
                        pe.wait_ge(s_whi, 3 * (i // 4 + 1))
                    ready(pe, s_silu, g - 1)
                    three(G_ps[k][:, :], wg_hi[:, c], wg_lo[:, c], xT_hi[p][:, :],
                          xT_lo[p][:, :]).then_inc(s_gate, 1)
                    ready(pe, s_h, g - 1)
                    three(U_ps[k][:, :], wu_hi[:, c], wu_lo[:, c], xT_hi[p][:, :],
                          xT_lo[p][:, :]).then_inc(s_up, 1)
                    if i >= LAG:
                        down(b, i - LAG)
                    elif not first:
                        down(b - 1, U + i - LAG)
                    if i < PAIRS:
                        if i == 0:
                            ready(pe, s_wT, b + 1)
                        ready(pe, s_h, g)
                        nc.tensor.matmul(W_ps[:, :], sel[:, c], wT[p][:, :], start=True,
                                         stop=True).then_inc(s_wb, 1)
                    if i in side and not last:
                        side[i](b + 1, 1 - p)

            pe.wait_ge(s_cst, 32)
            pe.wait_ge(s_setup_p, 2)
            pe.wait_ge(s_setup_d, 4)
            pe.wait_ge(s_setup_a, 3)
            transpose_xn(0, 0)
            pe.wait_ge(s_wshi, 1)
            pe.wait_ge(s_wslo, 1)
            for i in sorted(side)[1:]:
                side[i](0, 0)
            period(0, 0, first=True)
            with pe.Fori(0, (NBLK - 2) // 2) as j:
                period(2 * j + 1, 1)
                period(2 * j + 2, 0)
            period(NBLK - 1, 1, last=True)
            for i in range(U - LAG, U):
                down(NBLK - 1, i)

        @block.scalar
        def _(act):
            A = nc.scalar.activation

            def xT_parts(n, p):
                ready(act, s_xnT_ps, n + 1)
                A(xT_hi[p][:, :], SA[:, :], ACT.Copy).then_inc(s_xThi, 1)

            def exps(n, p):
                ready(act, s_ptok, n + 1)
                ready(act, s_w_tok, n)
                A(e_r[:, :, :], SBc[:, :, 0:E], ACT.Exp, scale=-1.0).then_inc(s_er, 1)
                ready(act, s_nabs, n + 1)
                A(sp_e[:, :], nabs[:, :], ACT.Exp).then_inc(s_spe, 1)
                ready(act, s_spe, n + 1)
                A(sp_l[:, :], sp_e[:, :], ACT.Ln, bias=1.0).then_inc(s_spl, 1)
                ready(act, s_Bs, n)
                A(B_tok[:, :, :], SBc[:, :, COL_B:COL_B + NS], ACT.Copy).then_inc(s_btok, 1)

            def bc_out(n, p):
                ready(act, s_pbc, n + 1)
                A(BT[:, :], SA[0:NS, :], ACT.Copy).then_inc(s_bt, 1)
                A(CT[:, :], SA[NS:2 * NS, :], ACT.Copy).then_inc(s_ct, 1)

            def decay_exps(n, p):
                ready(act, s_dec_ps, n + 1)
                A(dec[:, :], SB[:, 0:8], ACT.Exp).then_inc(s_dec, 1)
                A(ecum[:, :], SB[0:NS, C:T], ACT.Exp).then_inc(s_ecum, 1)
                ready(act, s_seg_ps, n + 1)
                A(Lt[:, :, :], SAc[:, :, :], ACT.Exp).then_inc(s_L, 1)

            def y_out(n, p):
                ready(act, s_y_ps, n + 1)
                A(yT[p][:, :], SA[:, :], ACT.Copy).then_inc(s_yT, 1)

            def w_out(n, p):
                ready(act, s_wT_ps, n + 1)
                A(wT[p][:, :], SB[0:2 * E, :], ACT.Copy).then_inc(s_wT, 1)

            side = {4: xT_parts, 7: exps, 8: bc_out, 11: decay_exps, 15: y_out, 16: w_out}

            def hi(b, i, p):
                g = U * b + i
                ready(act, s_h, g + 1)
                ready(act, s_down, g - HB + (1 if HB <= i < PAIRS else 0) if i < PAIRS else U * b)
                A(h_hi[slot(i)][:, :], hid[(p + i) % 2][:, :], ACT.Copy).then_inc(s_hi, 1)

            def period(b, p, first=False, last=False):
                for i in range(U):
                    g = U * b + i
                    k = (p + i) % 2
                    ready(act, s_gate, g + 1)
                    ready(act, s_h, g - 1)
                    A(sg[k][:, :], G_ps[k][:, :], ACT.Silu).then_inc(s_silu, 1)
                    if i > 0:
                        hi(b, i - 1, p)
                    elif not first:
                        hi(b - 1, U - 1, 1 - p)
                    if i == LAG and not first:
                        gate_out(b - 1)
                    if i in side and not last:
                        side[i](b + 1, 1 - p)

            def gate_out(b):
                ready(act, s_down, U * (b + 1))
                A(gate_o[:, :], O_ps[:, :], ACT.Silu).then_inc(s_go, 1)

            act.wait_ge(s_cst, 32)
            A(exp_a[:, :], par_sb[:, P_ALOG:P_ALOG + 1], ACT.Exp).then_inc(s_setup_a, 1)
            A(ident_b[:, :], ident, ACT.Copy).then_inc(s_setup_a, 1)
            A(sel[:, :].rearrange("k (e i) -> k e i", i=I),
              bc(cst[0:2 * E, K_EYE2:K_EYE2 + E].unsqueeze(2), [2 * E, E, I]), ACT.Copy).then_inc(s_setup_a, 1)
            act.wait_ge(s_wsm, 16)
            A(ws_hi[:, :], ws_raw[:, :], ACT.Copy).then_inc(s_wshi, 1)

            def split_hi(c):
                a, z = quarter(c)
                act.wait_ge(s_w[c], 48)
                for dst, src in ((wg_hi, wg_raw), (wu_hi, wu_raw), (wd_hi, wd_raw)):
                    A(dst[:, a:z], src[:, a:z], ACT.Copy).then_inc(s_whi, 1)

            xT_parts(0, 0)
            exps(0, 0)
            bc_out(0, 0)
            split_hi(0)
            decay_exps(0, 0)
            split_hi(1)
            split_hi(2)
            y_out(0, 0)
            w_out(0, 0)
            split_hi(3)
            period(0, 0, first=True)
            with act.Fori(0, (NBLK - 2) // 2) as j:
                period(2 * j + 1, 1)
                period(2 * j + 2, 0)
            period(NBLK - 1, 1, last=True)
            hi(NBLK - 1, U - 1, 1)
            gate_out(NBLK - 1)

        @block.vector
        def _(dve):
            V = nc.vector
            SIDE = 48
            count = [0]

            def step(n, ins, wait=True):
                count[0] += 1
                ins.then_inc(s_dve, 1)
                if wait:
                    dve.wait_ge(s_dve, SIDE * n + count[0])

            def stats_a(n, p, half):
                count[0] = 0
                ready(dve, s_xin[p], 16 * (half + 1))
                ready(dve, s_rstd, n)
                for t in range(2):
                    step(n, V.bn_stats(stats[:, t, :], xin[p][:, t, :]), wait=False)

            def stats_b(n, p, half):
                for t in range(2, NC_):
                    step(n, V.bn_stats(stats[:, t, :], xin[p][:, t, :]), wait=False)
                hold(dve, s_dve, SIDE * n + count[0])
                for t in range(NC_):
                    V.bn_aggr(mv[:, t, :], stats[:, t, :]).then_inc(s_stats, 1)

            def normalise(n, p, half):
                ready(dve, s_rstd, n + 1)
                ready(dve, s_y_ps, n)
                for t in range(NC_):
                    V.tensor_scalar(xn[:, t, :], xin[p][:, t, :], mv[:, t, 0:1], rstd[:, t:t + 1],
                                    ALU.subtract, ALU.mult).then_inc(s_xn, 1)

            def xT_low(n, p, half):
                ready(dve, s_xThi, n + 1)
                V.tensor_tensor(xT_lo[p][:, :], SA[:, :], xT_hi[p][:, :].bitcast(fp32),
                                ALU.subtract).then_inc(s_xTlo, 1)

            def softplus_in(n, p, half):
                ready(dve, s_ptok, n + 1)
                ready(dve, s_er, n + 1)
                step(n, V.tensor_scalar(zt[:, :], SBc[:, :, COL_DT:COL_DT + 1].rearrange("p t c -> p (t c)"),
                                        par_sb[:, P_DTB:P_DTB + 1], None, ALU.add))
                V.scalar_tensor_tensor(nabs[:, :], zt[:, :], -1.0, zt[:, :], ALU.mult, ALU.min).then_inc(s_nabs, 1)

            def route_scores(n, p, half):
                ready(dve, s_er, n + 1)
                step(n, V.tensor_scalar(r_p1[:, :, :], e_r[:, :, :], 1.0, None, ALU.add))
                step(n, V.reciprocal(score[:, :, :], r_p1[:, :, :]))
                step(n, V.tensor_tensor(sfc[:, :, :].rearrange("p (t g) e -> p t (g e)", g=NG), score[:, :, :],
                                        bc(par_sb[:, P_BIAS:P_BIAS + E].unsqueeze(1), [128, NC_, E]), ALU.add))

            def step_dt(n, p, half):
                ready(dve, s_spl, n + 1)
                step(n, V.scalar_tensor_tensor(dt_s[:, :], zt[:, :], 0.0, sp_l[:, :], ALU.max, ALU.add))
                V.tensor_scalar(dA[:, :], dt_s[:, :], neg_a[:, 0:1], None, ALU.mult).then_inc(s_dA, 1)

            def group_pairs(n, p, half):
                step(n, V.tensor_tensor(g4h[:, :, :], sfc[:, :, 0:4], sfc[:, :, 4:8], ALU.max))
                step(n, V.tensor_tensor(g4l[:, :, :], sfc[:, :, 0:4], sfc[:, :, 4:8], ALU.min))
                for h0, l0, h1, m1, x1, l1, k in ((g4h, g4l, g2h, g2m, g2x, g2l, 2), (g2h, g2l, g1h, g1m, g1x, g1l, 1)):
                    step(n, V.tensor_tensor(h1[:, :, :], h0[:, :, 0:k], h0[:, :, k:2 * k], ALU.max))
                    step(n, V.tensor_tensor(m1[:, :, :], h0[:, :, 0:k], h0[:, :, k:2 * k], ALU.min))
                    step(n, V.tensor_tensor(x1[:, :, :], l0[:, :, 0:k], l0[:, :, k:2 * k], ALU.max))
                    step(n, V.tensor_tensor(l1[:, :, :], m1[:, :, :], x1[:, :, :], ALU.max))
                step(n, V.tensor_tensor(gsum[:, :, :].rearrange("p t g -> p (t g)"), g1h[:, :, 0], g1l[:, :, 0], ALU.add))

            def group_rank(n, p, half):
                gi = bc(gsum[:, :, :].rearrange("p t g -> p (t g)").unsqueeze(2), [128, NC_ * NG, NG])
                gj = bc(gsum[:, :, :].unsqueeze(2), [128, NC_, NG, NG])
                gi = bc(gsum[:, :, :].unsqueeze(3), [128, NC_, NG, NG])
                v4 = lambda t_: t_[:, :, :].rearrange("p (t i) j -> p t i j", i=NG)
                step(n, V.tensor_tensor(v4(gt_ij), gj, gi, ALU.is_gt))
                step(n, V.tensor_tensor(v4(ge_ij), gj, gi, ALU.is_ge))
                step(n, V.tensor_tensor(gw_ij[:, :, :].rearrange("p a j -> p (a j)"),
                                        ge_ij[:, :, :].rearrange("p a j -> p (a j)"), beats_lm, ALU.mult))
                step(n, V.tensor_tensor(bt_ij[:, :, :], gw_ij[:, :, :], gt_ij[:, :, :], ALU.max))
                step(n, V.tensor_reduce(grank[:, :], bt_ij[:, :, :], axis=AXX, op=ALU.add))
                step(n, V.tensor_scalar(gkeep[:, :], grank[:, :], TOPG - 0.5, None, ALU.is_lt))
                step(n, V.tensor_tensor(cand[:, :, :], sfc[:, :, :], bc(gkeep[:, :].unsqueeze(2), [128, NC_ * NG, GE]),
                                        ALU.mult), wait=False)

            def top_experts(n, p, half):
                c4 = cand[:, :, :].rearrange("p (t g) e -> p t (g e)", g=NG)
                hold(dve, s_dve, SIDE * n + count[0])
                for t in range(NC_):
                    step(n, V.max(top8[:, t, :], c4[:, t, :]), wait=t == NC_ - 1)
                kth = bc(top8[:, :, TOPK - 1:TOPK], [128, NC_, E])
                step(n, V.tensor_tensor(above[:, :, :], c4, kth, ALU.is_gt))
                step(n, V.tensor_tensor(equal[:, :, :], c4, kth, ALU.is_equal))
                step(n, V.tensor_reduce(n_above[:, :], above[:, :, :], axis=AXX, op=ALU.add))
                step(n, V.tensor_scalar(room[:, :], n_above[:, :], -1.0, float(TOPK), ALU.mult, ALU.add))

            def ties(n, p, half):
                step(n, V.tensor_tensor_scan(nth[:, :], reset, equal[:, :, :].rearrange("p t e -> p (t e)"), 0.0,
                                             ALU.mult, ALU.add))
                step(n, V.tensor_tensor(fits[:, :, :], nth[:, :].rearrange("p (t e) -> p t e", e=E),
                                        bc(room[:, :].unsqueeze(2), [128, NC_, E]), ALU.is_le))
                step(n, V.tensor_tensor(tied[:, :, :], fits[:, :, :], equal[:, :, :], ALU.mult))
                step(n, V.tensor_tensor(chosen[:, :, :], tied[:, :, :], above[:, :, :], ALU.add))
                step(n, V.tensor_tensor(w0[:, :, :], chosen[:, :, :], score[:, :, :], ALU.mult))

            def weights(n, p, half):
                step(n, V.tensor_reduce(wsum[:, :], w0[:, :, :], axis=AXX, op=ALU.add))
                step(n, V.tensor_scalar(wsum_e[:, :], wsum[:, :], W_EPS, None, ALU.add))
                step(n, V.reciprocal(wrec[:, :], wsum_e[:, :]))
                step(n, V.scalar_tensor_tensor(wfull[:, :, :], w0[:, :, :], SCALE,
                                               bc(wrec[:, :].unsqueeze(2), [128, NC_, E]), ALU.mult, ALU.mult))
                step(n, V.tensor_copy(w_r[:, :, :], wfull[:, :, :]))
                ready(dve, s_wT_ps, n)
                step(n, V.tensor_copy(whl[:, :, 0:E], w_r[:, :, :].bitcast(fp32)))
                V.tensor_tensor(whl[:, :, E:2 * E], wfull[:, :, :], w_r[:, :, :].bitcast(fp32),
                                ALU.subtract).then_inc(s_w_tok, 1)

            def mask_scores(n, p, half):
                ready(dve, s_sc_ps, n + 1)
                ready(dve, s_L, n + 1)
                ready(dve, s_G, n)
                for t in range(NC_):
                    V.scalar_tensor_tensor(G0[:, t, :], SAc[:, t, :], dt_s[:, t:t + 1], Lt[:, t, :],
                                           ALU.mult, ALU.mult).then_inc(s_G0, 1)

            def states(n, p, half):
                ready(dve, s_st_ps, n + 1)
                ready(dve, s_dec, n + 1)
                step(n, V.tensor_copy(St[0][:, :], SB[0:NS, 0:C]))
                step(n, V.scalar_tensor_tensor(St[1][:, :], St[0][:, :], dec[0:NS, 5:6], SB[0:NS, C:2 * C],
                                               ALU.mult, ALU.add))
                V.scalar_tensor_tensor(St[2][:, :], St[1][:, :], dec[0:NS, 6:7], SB[0:NS, 2 * C:3 * C],
                                       ALU.mult, ALU.add).then_inc(s_S, 1)

            side = {0: [stats_a], 1: [stats_b], 3: [normalise], 5: [xT_low], 7: [softplus_in],
                    8: [step_dt, route_scores], 9: [group_pairs], 10: [group_rank], 11: [top_experts],
                    12: [ties], 13: [mask_scores, states], 14: [weights]}

            def final(b, p, half):
                ready(dve, s_go, b + 1)
                ready(dve, s_yT, b + 1)
                V.tensor_tensor(yg[:, :], yT[p][:, :], gate_o[:, :], ALU.mult).then_inc(s_yg, 1)
                ready(dve, s_yg, b + 1)
                ready(dve, s_xf[p], 16 * (half + 1))
                V.tensor_tensor(oT[p][:, :], yg[:, :], xf[p][:, :], ALU.add).then_inc(s_fin, 1)

            def period(b, p, half, first=False, last=False):
                other = half + (1 if p == 1 else 0)
                for i in range(U):
                    g = U * b + i
                    k = (p + i) % 2
                    ready(dve, s_silu, g + 1)
                    ready(dve, s_up, g + 1)
                    if i < PAIRS:
                        ready(dve, s_h, g - 1)
                        V.tensor_tensor(tt[k][:, :], sg[k][:, :], U_ps[k][:, :], ALU.mult).then_inc(s_t, 1)
                        ready(dve, s_t, PAIRS * b + i + 1)
                        ready(dve, s_wb, PAIRS * b + i + 1)
                        ready(dve, s_lo, g - 1)
                        V.tensor_tensor(hid[k][:, :], tt[k][:, :], W_ps[:, :], ALU.mult).then_inc(s_h, 1)
                    else:
                        ready(dve, s_lo, g - 1)
                        V.tensor_tensor(hid[k][:, :], sg[k][:, :], U_ps[k][:, :], ALU.mult).then_inc(s_h, 1)
                    if i == LAG and not first:
                        final(b - 1, 1 - p, half - (1 if p == 0 else 0))
                    if i in side and not last:
                        for s in side[i]:
                            s(b + 1, 1 - p, other)

            dve.wait_ge(s_cst, 32)
            V.tensor_scalar(negm_b[:, :].rearrange("p (t l) -> p t l", t=NC_),
                            bc(strict.unsqueeze(1), [128, NC_, 128]), NEG, None, ALU.mult).then_inc(s_setup_d, 1)
            V.tensor_scalar(d_ident[:, :], ident, par_sb[:, P_D:P_D + 1], None, ALU.mult).then_inc(s_setup_d, 1)
            dve.wait_ge(s_setup_a, 1)
            V.tensor_scalar(neg_a[:, :], exp_a[:, :], -1.0, None, ALU.mult).then_inc(s_setup_d, 1)
            V.memset(ones_r[:, :], 1.0).then_inc(s_setup_d, 1)
            dve.wait_ge(s_setup_d, 4)

            def split_lo(c):
                a, z = quarter(c)
                dve.wait_ge(s_whi, 3 * (c + 1))
                for dst, src, h in ((wg_lo, wg_raw, wg_hi), (wu_lo, wu_raw, wu_hi), (wd_lo, wd_raw, wd_hi)):
                    V.tensor_tensor(dst[:, a:z], src[:, a:z], h[:, a:z].bitcast(fp32),
                                    ALU.subtract).then_inc(s_wlo, 1)

            def prologue_side(stages):
                for i in stages:
                    for s in side[i]:
                        s(0, 0, 0)
            prologue_side([0, 1, 3])
            dve.wait_ge(s_wshi, 1)
            V.tensor_tensor(ws_lo[:, :], ws_raw[:, :], ws_hi[:, :].bitcast(fp32), ALU.subtract).then_inc(s_wslo, 1)
            prologue_side([5, 7, 8, 9, 10, 11, 12])
            split_lo(0)
            prologue_side([13, 14])
            assert count[0] == SIDE, count[0]
            split_lo(1)
            split_lo(2)
            split_lo(3)
            period(0, 0, 0, first=True)
            with dve.Fori(0, (NBLK - 2) // 2) as j:
                period(2 * j + 1, 1, j)
                period(2 * j + 2, 0, j + 1)
            period(NBLK - 1, 1, NBLK // 2 - 1, last=True)
            final(NBLK - 1, 1, NBLK // 2 - 1)

        @block.gpsimd
        def _(pool):
            P = nc.gpsimd

            def rstd_(n, p):
                ready(pool, s_stats, NC_ * (n + 1))
                ready(pool, s_xn, NC_ * n)
                P.tensor_tensor(var_eps[:, :], mv[:, :, 1], eps[:, :], ALU.add).then_inc(s_pool, 1)
                ready(pool, s_pool, 2 * n + 1)
                P.tensor_tensor(rstd[:, :], var_eps[:, :], halfpow[:, :], ALU.pow).then_inc(s_rstd, 1)

            def mask_dA(n, p):
                ready(pool, s_dA, n + 1)
                P.tensor_tensor(mk[:, :, :], bc(strict.unsqueeze(1), [128, NC_, 128]),
                                bc(dA[:, :].unsqueeze(2), [128, NC_, 128]), ALU.mult).then_inc(s_mk, 1)

            def scale_BC(n, p):
                ready(pool, s_dec, n + 1)
                P.tensor_tensor(dsdt[:, :], dec[:, 0:NC_], dt_s[:, :], ALU.mult).then_inc(s_pool, 1)
                ready(pool, s_pool, 2 * n + 2)
                ready(pool, s_btok, n + 1)
                P.tensor_tensor(Bs[:, :, :], B_tok[:, 0:NC_ - 1, :], bc(dsdt[:, 0:NC_ - 1].unsqueeze(2), [128, NC_ - 1, NS]),
                                ALU.mult).then_inc(s_Bs, 1)
                ready(pool, s_ecum, n + 1)
                ready(pool, s_ct, n + 1)
                P.tensor_tensor(CTs[:, :], CT[:, C:T], ecum[:, :], ALU.mult).then_inc(s_CTs, 1)

            def add_D(n, p):
                ready(pool, s_G0, NC_ * (n + 1))
                P.tensor_tensor(G[:, :, :], G0[:, :, :], bc(d_ident[:, :].unsqueeze(1), [128, NC_, 128]),
                                ALU.add).then_inc(s_G, 1)

            side = {2: rstd_, 9: mask_dA, 11: scale_BC, 13: add_D}

            def lo(b, i, p):
                g = U * b + i
                ready(pool, s_hi, g + 1)
                P.tensor_tensor(h_lo[slot(i)][:, :], hid[(p + i) % 2][:, :], h_hi[slot(i)][:, :].bitcast(fp32),
                                ALU.subtract).then_inc(s_lo, 1)

            def period(b, p, last=False):
                for i in range(U):
                    if i in side and not last:
                        side[i](b + 1, 1 - p)
                    lo(b, i, p)

            P.memset(halfpow[:, :], -0.5).then_inc(s_setup_p, 1)
            P.memset(eps[:, :], LN_EPS).then_inc(s_setup_p, 1)
            pool.wait_ge(s_setup_p, 2)
            pool.wait_ge(s_cst, 32)
            pool.wait_ge(s_setup_d, 4)
            for i in sorted(side):
                side[i](0, 0)
            period(0, 0)
            with pool.Fori(0, (NBLK - 2) // 2) as j:
                period(2 * j + 1, 1)
                period(2 * j + 2, 0)
            period(NBLK - 1, 1, last=True)


def _shape_constants(np):
    k = np.arange(128)
    c = np.zeros((128, K_END), np.float32)
    c[:, K_ID:K_ID + 128] = k[:, None] == k[None, :]
    c[:, K_TRI:K_TRI + 128] = k[:, None] <= k[None, :]
    c[:, K_STRICT:K_STRICT + 128] = k[:, None] > k[None, :]
    c[:, K_EYE2:K_EYE2 + E] = (k % E)[:, None] == np.arange(E)[None, :]
    g = np.arange(NG)
    c[:, K_BEATS:K_BEATS + NC_ * NG * NG] = np.tile((g[None, :] < g[:, None]).reshape(-1), NC_)
    c[:, K_RESET:K_RESET + NC_ * E] = np.arange(NC_ * E) % E != 0
    return c


def kernel(**inputs):
    import numpy as np
    import concourse.bacc as bacc
    from concourse import mybir as mb
    from concourse.bass_utils import run_bass_kernel_spmd as run

    a = {k: np.asarray(v) for k, v in inputs.items()}
    x = a["L0_attn_x"]
    wx = a["L0_attn_W_xproj"]
    feat = lambda w: w.reshape(-1, H).T
    gate = np.concatenate([feat(a["L0_ffn_gate_w"]), feat(a["L0_ffn_shared_gate_w"])], 1)
    up = np.concatenate([feat(a["L0_ffn_up_w"]), feat(a["L0_ffn_shared_up_w"])], 1)
    down = np.concatenate([a["L0_ffn_down_w"].transpose(0, 2, 1).reshape(E * I, H),
                           a["L0_ffn_shared_down_w"].T], 0)
    down = down.reshape(U, 128, H).transpose(1, 0, 2).reshape(128, U * H)
    small = np.concatenate([a["L0_ffn_router_weight"], wx[1:1 + NS], wx[0:1], wx[0:1], wx[1:]], 0).T
    row = np.concatenate([a["L0_ffn_router_bias"], a["L0_attn_dt_bias"], a["L0_attn_A_log"], a["L0_attn_D"]])
    arrays = {
        "x_tok": x.reshape(NBLK, NC_, C, H).transpose(0, 2, 1, 3),
        "x_feat": x.transpose(0, 2, 1),
        "w_gate": gate, "w_up": up, "w_down": down, "w_small": small,
        "consts": _shape_constants(np),
        "params": np.broadcast_to(row, (128, P_END)),
    }
    arrays = {k: np.ascontiguousarray(v) for k, v in arrays.items()}
    nc = bacc.Bacc("TRN2", target_bir_lowering=False, num_devices=1)
    args = [nc.dram_tensor(k, v.shape, mb.dt.from_np(v.dtype), kind="ExternalInput").ap() for k, v in arrays.items()]
    out = nc.dram_tensor("out", (NBLK, H, T), mb.dt.float32, kind="ExternalOutput").ap()
    gated_ssd_moe(nc, *args, out)
    r = run(nc, [arrays], core_ids=[0])
    return np.ascontiguousarray(np.asarray(r.results[0]["out"]).transpose(0, 2, 1))
```

```python
import concourse.bass as bass
from concourse import mybir
from contextlib import ExitStack

NBLK, T, H = 8, 512, 128
C = 128
NC_ = T // C
E, I = 32, 64
PAIRS = E // 2
QUARTERS, QP = 4, PAIRS // 4
U = PAIRS + 1
NS = 64
NG, GE = 4, E // 4
TOPG, TOPK = 2, 4
SCALE = 2.5
LN_EPS = 1e-5
W_EPS = 1e-20
NEG = -30000.0
WT = 98
COL_B, COL_DT = E, E + NS
LAG = 3
HB = 4

EXP_LN_SET = 6

K_ID, K_TRI, K_STRICT, K_BEATS, K_RESET, K_END = 0, 128, 256, 384, 448, 576
P_BIAS, P_DTB, P_ALOG, P_D, P_END = 0, E, E + 1, E + 2, E + 3


def gated_ssd_moe(nc, x_tok, x_feat, w_gate, w_up, w_down, w_small, consts, params, w_dram, out):
    fp32, f32r, bf16 = mybir.dt.float32, mybir.dt.float32r, mybir.dt.bfloat16
    ALU = mybir.AluOpType
    ACT = mybir.ActivationFunctionType
    AXX = mybir.AxisListType.X
    ctx = ExitStack()
    with ctx:
        def sb(name, shape, dt=fp32):
            return ctx.enter_context(nc.sbuf_tensor(name, shape, dt))

        def sem(name):
            return ctx.enter_context(nc.semaphore(name))

        wg_raw, wu_raw, wd_raw = (sb(n, [128, U * 128]) for n in ("wg_raw", "wu_raw", "wd_raw"))
        wg_hi, wu_hi, wd_hi = (sb(n, [128, U * 128], f32r) for n in ("wg_hi", "wu_hi", "wd_hi"))
        wg_lo, wu_lo, wd_lo = (sb(n, [128, U * 128], f32r) for n in ("wg_lo", "wu_lo", "wd_lo"))
        ws_raw = sb("ws_raw", [128, WT + 128])
        ws_hi = sb("ws_hi", [128, WT + 128], f32r)
        ws_lo = sb("ws_lo", [128, WT + 128], f32r)
        cst = sb("cst", [128, K_END])
        par_sb = sb("par_sb", [128, P_END])
        ones_r = sb("ones_r", [128, 128])
        halfpow = sb("halfpow", [128, NC_])
        eps = sb("eps", [128, NC_])
        ident_b = sb("ident_b", [128, 128], bf16)
        negm_b = sb("negm_b", [128, NC_ * 128], bf16)
        d_ident = sb("d_ident", [128, 128])
        neg_a = sb("neg_a", [128, 1])
        exp_a = sb("exp_a", [128, 1])
        ident = cst[:, K_ID:K_ID + 128]
        tri = cst[:, K_TRI:K_TRI + 128]
        strict = cst[:, K_STRICT:K_STRICT + 128]
        beats_lm = cst[:, K_BEATS:K_BEATS + NC_ * NG * NG]
        reset = cst[:, K_RESET:K_RESET + NC_ * E]

        xin = [sb(f"xin{k}", [128, NC_, H]) for k in range(2)]
        xf = [sb(f"xf{k}", [128, T]) for k in range(2)]
        xT_hi = [sb(f"xT_hi{k}", [128, T], f32r) for k in range(2)]
        xT_lo = [sb(f"xT_lo{k}", [128, T], f32r) for k in range(2)]
        wT = sb("wT", [E, T])
        wrow = [sb(f"wrow{q}", [128, QP, T]) for q in range(QUARTERS)]
        yT = [sb(f"yT{k}", [128, T]) for k in range(2)]
        oT = [sb(f"oT{k}", [128, T]) for k in range(2)]
        stats = sb("stats", [128, NC_, 6])
        mv = sb("mv", [128, NC_, 2])
        var_eps = sb("var_eps", [128, NC_])
        rstd = sb("rstd", [128, NC_])
        xn = sb("xn", [128, NC_, H])
        z_pos = sb("z_pos", [128, NC_])
        z_abs = sb("z_abs", [128, NC_])
        sp_e = sb("sp_e", [128, NC_])
        sp_l = sb("sp_l", [128, NC_])
        dt_s = sb("dt_s", [128, NC_])
        dA = sb("dA", [128, NC_])
        mk = sb("mk", [128, NC_, 128])
        Lt = sb("Lt", [128, NC_, 128])
        dec = sb("dec", [128, 8])
        ecum = sb("ecum", [64, 3 * 128])
        dsdt = sb("dsdt", [128, NC_])
        B_tok = sb("B_tok", [128, NC_, NS])
        Bs = sb("Bs", [128, 3, NS])
        BT = sb("BT", [64, T])
        CT = sb("CT", [64, T])
        CTs = sb("CTs", [64, 3 * 128])
        G0 = sb("G0", [128, NC_, 128])
        G = sb("G", [128, NC_, 128])
        St = [sb(f"St{k}", [64, H]) for k in range(3)]
        e_r = sb("e_r", [128, NC_, E])
        r_p1 = sb("r_p1", [128, NC_, E])
        score = sb("score", [128, NC_, E])
        sfc = sb("sfc", [128, NC_ * NG, GE + GE // 2])
        pair_sum = sb("pair_sum", [128, NC_ * NG, GE // 2 * GE])
        gsum = sb("gsum", [128, NC_, NG])
        gt_ij, ge_ij, gw_ij, bt_ij = (sb(f"{n}_ij", [128, NC_ * NG, NG]) for n in ("gt", "ge", "gw", "bt"))
        grank = sb("grank", [128, NC_ * NG])
        cand = sb("cand", [128, NC_ * NG, GE])
        top8 = sb("top8", [128, NC_, 8])
        above = sb("above", [128, NC_, E])
        equal = sb("equal", [128, NC_, E])
        n_above = sb("n_above", [128, NC_])
        room = sb("room", [128, NC_])
        nth = sb("nth", [128, NC_ * E])
        fits = sb("fits", [128, NC_, E])
        tied = sb("tied", [128, NC_, E])
        chosen = sb("chosen", [128, NC_, E])
        w0 = sb("w0", [128, NC_, E])
        wsum = sb("wsum", [128, NC_])
        wsum_e = sb("wsum_e", [128, NC_])
        wrec = sb("wrec", [128, NC_])
        wfull = sb("wfull", [128, NC_, E])
        sg = [sb(f"sg{k}", [128, T]) for k in range(2)]
        tt = [sb(f"tt{k}", [128, T]) for k in range(2)]
        hid = [sb(f"hid{k}", [128, T]) for k in range(2)]
        h_hi = [sb(f"h_hi{k}", [128, T], f32r) for k in range(HB + 1)]
        h_lo = [sb(f"h_lo{k}", [128, T], f32r) for k in range(HB + 1)]
        gate_o = sb("gate_o", [128, T])

        def bank(name):
            return ctx.enter_context(nc.psum_tensor(name, [128, T], fp32))
        G_ps = [bank("G0_ps"), bank("G1_ps")]
        U_ps = [bank("U0_ps"), bank("U1_ps")]
        O_ps, SA, SB, SC = bank("O_ps"), bank("SA"), bank("SB"), bank("SC")
        SAc, SBc, SCc = (x[:, :].rearrange("p (t c) -> p t c", t=NC_) for x in (SA, SB, SC))

        s_cst = sem("s_cst")
        s_wsm = sem("s_wsm")
        s_w = [sem(f"s_w{c}") for c in range(4)]
        s_xin = [sem(f"s_xin{k}") for k in range(2)]
        s_xf = [sem(f"s_xf{k}") for k in range(2)]
        s_setup_p = sem("s_setup_p")
        s_setup_a = sem("s_setup_a")
        s_setup_d = sem("s_setup_d")
        s_wshi = sem("s_wshi")
        s_wslo = sem("s_wslo")
        s_whi = sem("s_whi")
        s_wlo = sem("s_wlo")
        s_dve = sem("s_dve")
        s_pool = sem("s_pool")
        s_top = sem("s_top")
        s_stats = sem("s_stats")
        s_rstd = sem("s_rstd")
        s_xn = sem("s_xn")
        s_xnT_ps = sem("s_xnT_ps")
        s_xThi = sem("s_xThi")
        s_xTlo = sem("s_xTlo")
        s_ptok = sem("s_ptok")
        s_pbc = sem("s_pbc")
        s_zabs = sem("s_zabs")
        s_spe = sem("s_spe")
        s_spl = sem("s_spl")
        s_er = sem("s_er")
        s_btok = sem("s_btok")
        s_bt = sem("s_bt")
        s_ct = sem("s_ct")
        s_dt = sem("s_dt")
        s_dA = sem("s_dA")
        s_mk = sem("s_mk")
        s_dec_ps = sem("s_dec_ps")
        s_seg_ps = sem("s_seg_ps")
        s_L = sem("s_L")
        s_dec = sem("s_dec")
        s_ecum = sem("s_ecum")
        s_Bs = sem("s_Bs")
        s_CTs = sem("s_CTs")
        s_sc_ps = sem("s_sc_ps")
        s_st_ps = sem("s_st_ps")
        s_G0 = sem("s_G0")
        s_G = sem("s_G")
        s_S = sem("s_S")
        s_y_ps = sem("s_y_ps")
        s_yT = sem("s_yT")
        s_w_tok = sem("s_w_tok")
        s_wT_ps = sem("s_wT_ps")
        s_wT = sem("s_wT")
        s_gate = sem("s_gate")
        s_up = sem("s_up")
        s_wdram = [sem(f"s_wdram{k}") for k in range(2)]
        s_wrow = [sem(f"s_wrow{q}") for q in range(QUARTERS)]
        s_silu = sem("s_silu")
        s_t = sem("s_t")
        s_h = sem("s_h")
        s_hi = sem("s_hi")
        s_lo = sem("s_lo")
        s_down = sem("s_down")
        s_go = sem("s_go")
        s_yg = sem("s_yg")
        s_fin = sem("s_fin")
        s_held = sem("s_held")
        s_out = [sem(f"s_out{k}") for k in range(2)]

        def ready(eng, semaphore, value):
            if isinstance(value, int) and value <= 0:
                return
            eng.wait_ge(semaphore, value)

        def hold(eng, semaphore, value):
            eng.wait_ge(semaphore, value)
            eng.sem_inc(s_held, 1)

        def bc(ap, shape):
            return ap.to_broadcast(shape)

        def slot(i):
            return i % HB if i < PAIRS else HB

        def quarter(c):
            return c * 4 * 128, (c + 1) * 4 * 128 if c < 3 else U * 128

        block = ctx.enter_context(nc.Block())

        def store(sp, b):
            ready(sp, s_fin, b + 1)
            sp.dma_start(out[b], oT[b % 2][:, :]).then_inc(s_out[b % 2], 16)
            if b + 2 < NBLK:
                sp.wait_ge(s_out[b % 2], 16 * (b // 2 + 1))
                sp.dma_start(xf[b % 2][:, :], x_feat[b + 2]).then_inc(s_xf[b % 2], 16)

        @block.sync
        def _(sp):
            def spread_weights(n):
                k = n % 2
                ready(sp, s_wT, n + 1)
                sp.dma_start(w_dram[k], wT[:, :]).then_inc(s_wdram[k], 16)
                sp.wait_ge(s_wdram[k], 16 * (n // 2 + 1))
                for q in range(QUARTERS):
                    ready(sp, s_h, U * (n - 1) + (q + 1) * QP)
                    for half in range(2):
                        e0 = half * PAIRS + q * QP
                        rows = w_dram[k, e0:e0 + QP, :].rearrange("e t -> (e t)").unsqueeze(0)
                        sp.dma_start(wrow[q][half * I:(half + 1) * I, :, :].rearrange("p e t -> p (e t)"),
                                     rows.to_broadcast([I, QP * T])).then_inc(s_wrow[q], 16)

            sp.dma_start(xin[0][:, :, :], x_tok[0]).then_inc(s_xin[0], 16)
            sp.dma_start(cst[:, :], consts[:, :]).then_inc(s_cst, 16)
            sp.dma_start(par_sb[:, :], params[:, :]).then_inc(s_cst, 16)
            sp.dma_start(ws_raw[:, :], w_small[:, :]).then_inc(s_wsm, 16)
            for c in range(4):
                a, z = quarter(c)
                for dst, src in ((wg_raw, w_gate), (wu_raw, w_up), (wd_raw, w_down)):
                    sp.dma_start(dst[:, a:z], src[:, a:z]).then_inc(s_w[c], 16)
                if c == 0:
                    sp.dma_start(xin[1][:, :, :], x_tok[1]).then_inc(s_xin[1], 16)
            for k in range(2):
                sp.dma_start(xf[k][:, :], x_feat[k]).then_inc(s_xf[k], 16)
            spread_weights(0)
            for b in range(NBLK):
                if b + 2 < NBLK:
                    ready(sp, s_xn, NC_ * (b + 1))
                    sp.dma_start(xin[b % 2][:, :, :], x_tok[b + 2]).then_inc(s_xin[b % 2], 16)
                if b > 0:
                    store(sp, b - 1)
                if b + 1 < NBLK:
                    spread_weights(b + 1)
            store(sp, NBLK - 1)
            for k in range(2):
                sp.wait_ge(s_out[k], 16 * NBLK // 2)

        @block.tensor
        def _(pe):
            def three(ps, a_hi, a_lo, x_hi, x_lo):
                nc.tensor.matmul(ps, a_lo, x_hi, start=True, stop=False)
                nc.tensor.matmul(ps, a_hi, x_lo, start=False, stop=False)
                return nc.tensor.matmul(ps, a_hi, x_hi, start=False, stop=True)

            def transpose_xn(n, p):
                ready(pe, s_xn, NC_ * (n + 1))
                ready(pe, s_S, n)
                for t in range(NC_):
                    m = nc.tensor.transpose(SAc[:, t, :], xn[:, t, :], ident)
                m.then_inc(s_xnT_ps, 1)

            def project(n, p):
                ready(pe, s_xTlo, n + 1)
                ready(pe, s_yT, n)
                for t in range(NC_):
                    c = slice(t * C, (t + 1) * C)
                    m = three(SBc[:, t, 0:WT], xT_hi[p][:, c], xT_lo[p][:, c],
                              ws_hi[:, 0:WT], ws_lo[:, 0:WT])
                m.then_inc(s_ptok, 1)
                ready(pe, s_G0, NC_ * n)
                three(SC[:, :], ws_hi[:, WT:WT + 128], ws_lo[:, WT:WT + 128],
                      xT_hi[p][:, :], xT_lo[p][:, :]).then_inc(s_pbc, 1)

            def decays(n, p):
                ready(pe, s_dA, n + 1)
                nc.tensor.matmul(SA[:, 0:NC_], strict, dA[:, :], start=True, stop=True)
                nc.tensor.matmul(SA[:, NC_:2 * NC_], ones_r[:, :], dA[:, :], start=True, stop=True)
                for t in range(1, NC_):
                    m = nc.tensor.matmul(SA[0:NS, t * C:(t + 1) * C], bc(dA[:, t:t + 1], [128, NS]), tri,
                                         start=True, stop=True)
                m.then_inc(s_dec_ps, 1)
                ready(pe, s_mk, n + 1)
                nc.tensor.matmul(SB[:, :], ident_b[:, :], negm_b[:, :], start=True, stop=False)
                for t in range(NC_):
                    m = nc.tensor.matmul(SBc[:, t, :], mk[:, t, :], tri, start=False, stop=t == NC_ - 1)
                m.then_inc(s_seg_ps, 1)

            def transpose_w(n, p):
                ready(pe, s_w_tok, n + 1)
                hold(pe, s_L, n + 1)
                for t in range(NC_):
                    m = nc.tensor.transpose(SB[0:E, t * C:(t + 1) * C], wfull[:, t, :], ident)
                m.then_inc(s_wT_ps, 1)

            def scores(n, p):
                ready(pe, s_ct, n + 1)
                for t in range(NC_):
                    c = slice(t * C, (t + 1) * C)
                    m = nc.tensor.matmul(SCc[:, t, :], BT[:, c], CT[:, c], start=True, stop=True)
                m.then_inc(s_sc_ps, 1)
                ready(pe, s_ecum, n + 1)
                ready(pe, s_Bs, n + 1)
                for t in range(NC_ - 1):
                    m = nc.tensor.matmul(SA[0:NS, t * C:(t + 1) * C], Bs[:, t, :], xn[:, t, :],
                                         start=True, stop=True)
                m.then_inc(s_st_ps, 1)

            def mix(n, p):
                ready(pe, s_G, n + 1)
                ready(pe, s_S, n + 1)
                ready(pe, s_CTs, n + 1)
                ready(pe, s_wT, n + 1)
                for t in range(NC_):
                    m = nc.tensor.matmul(SBc[:, t, :], xn[:, t, :], G[:, t, :], start=True, stop=t == 0)
                    if t > 0:
                        m = nc.tensor.matmul(SBc[:, t, :], St[t - 1][:, :], CTs[:, (t - 1) * C:t * C],
                                             start=False, stop=True)
                m.then_inc(s_y_ps, 1)

            side = {2: transpose_xn, 5: project, 9: decays, 12: scores, 13: transpose_w, 15: mix}

            def down(b, i):
                g = U * b + i
                if i == 0:
                    ready(pe, s_go, b)
                ready(pe, s_lo, g + 1)
                c = slice(i * 128, (i + 1) * 128)
                s = slot(i)
                nc.tensor.matmul(O_ps[:, :], wd_lo[:, c], h_hi[s][:, :], start=i == 0, stop=False)
                nc.tensor.matmul(O_ps[:, :], wd_hi[:, c], h_lo[s][:, :], start=False, stop=False)
                nc.tensor.matmul(O_ps[:, :], wd_hi[:, c], h_hi[s][:, :], start=False,
                                 stop=i == U - 1).then_inc(s_down, 1)

            def period(b, p, first=False, last=False):
                for i in range(U):
                    g = U * b + i
                    k = (p + i) % 2
                    c = slice(i * 128, (i + 1) * 128)
                    if first and i % 4 == 0 and i < PAIRS:
                        pe.wait_ge(s_wlo, 3 * (i // 4 + 1))
                    ready(pe, s_silu, g - 1)
                    three(G_ps[k][:, :], wg_hi[:, c], wg_lo[:, c], xT_hi[p][:, :],
                          xT_lo[p][:, :]).then_inc(s_gate, 1)
                    ready(pe, s_h, g - 1)
                    three(U_ps[k][:, :], wu_hi[:, c], wu_lo[:, c], xT_hi[p][:, :],
                          xT_lo[p][:, :]).then_inc(s_up, 1)
                    if i >= LAG:
                        down(b, i - LAG)
                    elif not first:
                        down(b - 1, U + i - LAG)
                    if i in side and not last:
                        side[i](b + 1, 1 - p)

            pe.wait_ge(s_cst, 32)
            pe.wait_ge(s_setup_p, 2)
            pe.wait_ge(s_setup_d, 4)
            pe.wait_ge(s_setup_a, 2)
            transpose_xn(0, 0)
            pe.wait_ge(s_wshi, 1)
            pe.wait_ge(s_wslo, 1)
            for i in sorted(side)[1:]:
                side[i](0, 0)
            period(0, 0, first=True)
            with pe.Fori(0, (NBLK - 2) // 2) as j:
                period(2 * j + 1, 1)
                period(2 * j + 2, 0)
            period(NBLK - 1, 1, last=True)
            for i in range(U - LAG, U):
                down(NBLK - 1, i)

        @block.scalar
        def _(act):
            A = nc.scalar.activation

            def xT_parts(n, p):
                ready(act, s_xnT_ps, n + 1)
                A(xT_hi[p][:, :], SA[:, :], ACT.Copy).then_inc(s_xThi, 1)

            def load_exp_ln():
                nc.scalar.add_instruction(mybir.InstLoadActFuncSet(
                    name=nc.get_next_instruction_name(), engine=mybir.EngineType.Activation,
                    act_func_set_id=EXP_LN_SET))

            def exps(n, p):
                ready(act, s_ptok, n + 1)
                ready(act, s_dA, n)
                ready(act, s_Bs, n)
                A(B_tok[:, :, :], SBc[:, :, COL_B:COL_B + NS], ACT.Copy).then_inc(s_btok, 1)
                A(z_abs[:, :], SBc[:, :, COL_DT], ACT.Abs, bias=par_sb[:, P_DTB:P_DTB + 1]).then_inc(s_zabs, 1)
                load_exp_ln()
                ready(act, s_w_tok, n)
                A(e_r[:, :, :], SBc[:, :, 0:E], ACT.Exp, scale=-1.0).then_inc(s_er, 1)
                ready(act, s_zabs, n + 1)
                A(sp_e[:, :], z_abs[:, :], ACT.Exp, scale=-1.0).then_inc(s_spe, 1)
                ready(act, s_spe, n + 1)
                A(sp_l[:, :], sp_e[:, :], ACT.Ln, bias=1.0).then_inc(s_spl, 1)

            def bc_out(n, p):
                ready(act, s_pbc, n + 1)
                A(BT[:, :], SC[0:NS, :], ACT.Copy).then_inc(s_bt, 1)
                A(CT[:, :], SC[NS:2 * NS, :], ACT.Copy).then_inc(s_ct, 1)

            def decay_exps(n, p):
                ready(act, s_dec_ps, n + 1)
                A(dec[:, :], SA[:, 0:8], ACT.Exp).then_inc(s_dec, 1)
                A(ecum[:, :], SA[0:NS, C:T], ACT.Exp).then_inc(s_ecum, 1)
                ready(act, s_seg_ps, n + 1)
                A(Lt[:, :, :], SBc[:, :, :], ACT.Exp).then_inc(s_L, 1)

            def w_out(n, p):
                ready(act, s_wT_ps, n + 1)
                A(wT[:, :], SB[0:E, :], ACT.Copy).then_inc(s_wT, 1)

            def y_out(n, p):
                ready(act, s_y_ps, n + 1)
                A(yT[p][:, :], SB[:, :], ACT.Copy).then_inc(s_yT, 1)

            side = {3: xT_parts, 6: exps, 7: bc_out, 10: decay_exps, 14: w_out, 16: y_out}

            def hi(b, i, p):
                g = U * b + i
                ready(act, s_h, g + 1)
                ready(act, s_down, g - HB + (1 if HB <= i < PAIRS else 0) if i < PAIRS else U * b)
                A(h_hi[slot(i)][:, :], hid[(p + i) % 2][:, :], ACT.Copy).then_inc(s_hi, 1)

            def split_hi(c, k):
                a, z = quarter(c)
                act.wait_ge(s_w[c], 48)
                dst, src = ((wg_hi, wg_raw), (wu_hi, wu_raw), (wd_hi, wd_raw))[k]
                A(dst[:, a:z], src[:, a:z], ACT.Copy).then_inc(s_whi, 1)

            def period(b, p, first=False, last=False):
                for i in range(U):
                    g = U * b + i
                    k = (p + i) % 2
                    if first and i < 9:
                        split_hi(1 + i // 3, i % 3)
                    if i == LAG and not first:
                        gate_out(b - 1)
                    ready(act, s_gate, g + 1)
                    ready(act, s_h, g - 1)
                    A(sg[k][:, :], G_ps[k][:, :], ACT.Silu).then_inc(s_silu, 1)
                    if i > 0:
                        hi(b, i - 1, p)
                    elif not first:
                        hi(b - 1, U - 1, 1 - p)
                    if i in side and not last:
                        side[i](b + 1, 1 - p)

            def gate_out(b):
                ready(act, s_down, U * (b + 1))
                A(gate_o[:, :], O_ps[:, :], ACT.Silu).then_inc(s_go, 1)

            act.wait_ge(s_cst, 32)
            A(exp_a[:, :], par_sb[:, P_ALOG:P_ALOG + 1], ACT.Exp).then_inc(s_setup_a, 1)
            A(ident_b[:, :], ident, ACT.Copy).then_inc(s_setup_a, 1)
            act.wait_ge(s_wsm, 16)
            A(ws_hi[:, :], ws_raw[:, :], ACT.Copy).then_inc(s_wshi, 1)

            xT_parts(0, 0)
            split_hi(0, 0)
            exps(0, 0)
            bc_out(0, 0)
            split_hi(0, 1)
            split_hi(0, 2)
            decay_exps(0, 0)
            w_out(0, 0)
            y_out(0, 0)
            period(0, 0, first=True)
            with act.Fori(0, (NBLK - 2) // 2) as j:
                period(2 * j + 1, 1)
                period(2 * j + 2, 0)
            period(NBLK - 1, 1, last=True)
            hi(NBLK - 1, U - 1, 1)
            gate_out(NBLK - 1)

        @block.vector
        def _(dve):
            V = nc.vector
            SIDE = 32
            count = [0]

            def step(n, make, *args, wait=True, **kw):
                if wait:
                    ready(dve, s_dve, SIDE * n + count[0])
                count[0] += 1
                return make(*args, **kw).then_inc(s_dve, 1)

            def stats_a(n, p, half):
                count[0] = 0
                ready(dve, s_xin[p], 16 * (half + 1))
                ready(dve, s_rstd, n)
                for t in range(NC_):
                    step(n, V.bn_stats, stats[:, t, :], xin[p][:, t, :], wait=False)

            def stats_b(n, p, half):
                hold(dve, s_dve, SIDE * n + count[0])
                for t in range(NC_):
                    V.bn_aggr(mv[:, t, :], stats[:, t, :]).then_inc(s_stats, 1)

            def normalise(n, p, half):
                ready(dve, s_rstd, n + 1)
                ready(dve, s_y_ps, n)
                for t in range(NC_):
                    V.tensor_scalar(xn[:, t, :], xin[p][:, t, :], mv[:, t, 0:1], rstd[:, t:t + 1],
                                    ALU.subtract, ALU.mult).then_inc(s_xn, 1)

            def xT_low(n, p, half):
                ready(dve, s_xThi, n + 1)
                V.tensor_tensor(xT_lo[p][:, :], SA[:, :], xT_hi[p][:, :].bitcast(fp32),
                                ALU.subtract).then_inc(s_xTlo, 1)

            def softplus(n, p, half):
                ready(dve, s_er, n + 1)
                step(n, V.tensor_scalar, z_pos[:, :], SBc[:, :, COL_DT], par_sb[:, P_DTB:P_DTB + 1], 0.0,
                     ALU.add, ALU.max, wait=False)
                ready(dve, s_spl, n + 1)
                step(n, V.tensor_tensor, dt_s[:, :], z_pos[:, :], sp_l[:, :], ALU.add)
                ready(dve, s_dve, SIDE * n + count[0])
                V.tensor_scalar(dA[:, :], dt_s[:, :], neg_a[:, 0:1], None, ALU.mult).then_inc(s_dA, 1)

            def score_a(n, p, half):
                ready(dve, s_er, n + 1)
                step(n, V.tensor_scalar, r_p1[:, :, :], e_r[:, :, :], 1.0, None, ALU.add, wait=False)
                step(n, V.reciprocal, score[:, :, :], r_p1[:, :, :])

            def score_b(n, p, half):
                s16 = score[:, :, :].rearrange("p t (g e) -> p t g e", g=NG)
                b16 = par_sb[:, P_BIAS:P_BIAS + E].rearrange("p (g e) -> p g e", g=NG)
                sf = sfc[:, :, :].rearrange("p (t g) e -> p t g e", g=NG)
                bb = bc(b16.unsqueeze(1), [128, NC_, NG, GE])
                step(n, V.tensor_tensor, sf[:, :, :, 0:GE], s16, bb, ALU.add)
                step(n, V.tensor_tensor, sf[:, :, :, GE:GE + GE // 2], s16[:, :, :, 0:GE // 2],
                     bb[:, :, :, 0:GE // 2], ALU.add, wait=False)

            def group_a(n, p, half):
                near = bc(sfc[:, :, 0:GE].unsqueeze(2), [128, NC_ * NG, GE // 2, GE])
                step(n, V.tensor_tensor, pair_sum[:, :, :].rearrange("p a (d e) -> p a d e", e=GE), near, far(),
                     ALU.add)
                step(n, V.tensor_reduce, gsum[:, :, :].rearrange("p t g -> p (t g)"), pair_sum[:, :, :],
                     axis=AXX, op=ALU.max)

            def far():
                v = sfc[:, :, 1:1 + GE].unsqueeze(2)
                w = bc(v, [128, NC_ * NG, GE // 2, GE])
                ap = [list(x) for x in w.ap]
                ap[2][0] = 1
                return bass.AP(tensor=w.tensor, offset=w.offset, ap=ap)

            def rank_a(n, p, half):
                gj = bc(gsum[:, :, :].unsqueeze(2), [128, NC_, NG, NG])
                gi = bc(gsum[:, :, :].unsqueeze(3), [128, NC_, NG, NG])
                v4 = lambda t_: t_[:, :, :].rearrange("p (t i) j -> p t i j", i=NG)
                step(n, V.tensor_tensor, v4(ge_ij), gj, gi, ALU.is_ge)
                step(n, V.tensor_tensor, v4(gt_ij), gj, gi, ALU.is_gt, wait=False)

            def rank_b(n, p, half):
                flat = lambda t_: t_[:, :, :].rearrange("p a j -> p (a j)")
                step(n, V.tensor_tensor, flat(gw_ij), flat(ge_ij), beats_lm, ALU.mult)
                step(n, V.tensor_tensor, flat(bt_ij), flat(gw_ij), flat(gt_ij), ALU.max)

            def rank_c(n, p, half):
                step(n, V.tensor_reduce, grank[:, :], bt_ij[:, :, :], axis=AXX, op=ALU.add)
                step(n, V.scalar_tensor_tensor, cand[:, :, :], bc(grank[:, :].unsqueeze(2), [128, NC_ * NG, GE]),
                     TOPG - 0.5, sfc[:, :, 0:GE], ALU.is_lt, ALU.mult)

            c4 = cand[:, :, :].rearrange("p (t g) e -> p t (g e)", g=NG)

            def top_a(n, p, half):
                hold(dve, s_dve, SIDE * n + count[0])
                for t in range(NC_):
                    V.max(top8[:, t, :], c4[:, t, :]).then_inc(s_top, 1)

            def top_b(n, p, half):
                kth = bc(top8[:, :, TOPK - 1:TOPK], [128, NC_, E])
                ready(dve, s_top, NC_ * (n + 1))
                step(n, V.tensor_tensor, above[:, :, :], c4, kth, ALU.is_gt, wait=False)
                step(n, V.tensor_tensor, equal[:, :, :], c4, kth, ALU.is_equal, wait=False)

            def top_c(n, p, half):
                step(n, V.tensor_reduce, n_above[:, :], above[:, :, :], axis=AXX, op=ALU.add)
                step(n, V.tensor_tensor_scan, nth[:, :], reset, equal[:, :, :].rearrange("p t e -> p (t e)"), 0.0,
                     ALU.mult, ALU.add, wait=False)
                ready(dve, s_dve, SIDE * n + count[0] - 1)
                step(n, V.tensor_scalar, room[:, :], n_above[:, :], -1.0, float(TOPK), ALU.mult, ALU.add, wait=False)

            def ties_a(n, p, half):
                step(n, V.tensor_tensor, fits[:, :, :], nth[:, :].rearrange("p (t e) -> p t e", e=E),
                     bc(room[:, :].unsqueeze(2), [128, NC_, E]), ALU.is_le)
                step(n, V.tensor_tensor, tied[:, :, :], fits[:, :, :], equal[:, :, :], ALU.mult)

            def ties_b(n, p, half):
                step(n, V.tensor_tensor, chosen[:, :, :], tied[:, :, :], above[:, :, :], ALU.add)
                step(n, V.tensor_tensor, w0[:, :, :], chosen[:, :, :], score[:, :, :], ALU.mult)

            def weights_a(n, p, half):
                step(n, V.tensor_reduce, wsum[:, :], w0[:, :, :], axis=AXX, op=ALU.add)
                step(n, V.tensor_scalar, wsum_e[:, :], wsum[:, :], W_EPS, None, ALU.add)

            def weights_b(n, p, half):
                step(n, V.reciprocal, wrec[:, :], wsum_e[:, :])
                ready(dve, s_dve, SIDE * n + count[0])
                V.scalar_tensor_tensor(wfull[:, :, :], w0[:, :, :], SCALE, bc(wrec[:, :].unsqueeze(2), [128, NC_, E]),
                                       ALU.mult, ALU.mult).then_inc(s_w_tok, 1)

            def mask_scores(n, p, half):
                ready(dve, s_sc_ps, n + 1)
                ready(dve, s_L, n + 1)
                ready(dve, s_G, n)
                for t in range(NC_):
                    V.scalar_tensor_tensor(G0[:, t, :], SCc[:, t, :], dt_s[:, t:t + 1], Lt[:, t, :],
                                           ALU.mult, ALU.mult).then_inc(s_G0, 1)

            def states_a(n, p, half):
                ready(dve, s_st_ps, n + 1)
                ready(dve, s_dec, n + 1)
                step(n, V.tensor_copy, St[0][:, :], SA[0:NS, 0:C], wait=False)
                step(n, V.scalar_tensor_tensor, St[1][:, :], St[0][:, :], dec[0:NS, 5:6], SA[0:NS, C:2 * C],
                     ALU.mult, ALU.add)

            def states_b(n, p, half):
                ready(dve, s_dve, SIDE * n + count[0])
                V.scalar_tensor_tensor(St[2][:, :], St[1][:, :], dec[0:NS, 6:7], SA[0:NS, 2 * C:3 * C],
                                       ALU.mult, ALU.add).then_inc(s_S, 1)

            side = {0: ([stats_a, stats_b], [normalise]), 3: ([], [xT_low]), 6: ([], [softplus, score_a]),
                    7: ([score_b], [group_a]), 8: ([rank_a], [rank_b]), 9: ([rank_c], [top_a, top_b]),
                    10: ([top_c], [ties_a]), 11: ([ties_b, weights_a], [weights_b]),
                    12: ([], [mask_scores, states_a]), 13: ([states_b], [])}

            def period(b, p, half, first=False, last=False):
                other = half + (1 if p == 1 else 0)
                for i in range(U):
                    g = U * b + i
                    k = (p + i) % 2
                    before, after = side.get(i, ([], [])) if not last else ([], [])
                    if first and i < 9:
                        split_lo(1 + i // 3, i % 3)
                    ready(dve, s_silu, g + 1)
                    ready(dve, s_up, g + 1)
                    if i < PAIRS:
                        ready(dve, s_h, g - 1)
                        V.tensor_tensor(tt[k][:, :], sg[k][:, :], U_ps[k][:, :], ALU.mult).then_inc(s_t, 1)
                        for s in before:
                            s(b + 1, 1 - p, other)
                        if i % QP == 0:
                            ready(dve, s_wrow[i // QP], 32 * (b + 1))
                        ready(dve, s_t, PAIRS * b + i + 1)
                        ready(dve, s_lo, g - 1)
                        V.tensor_tensor(hid[k][:, :], tt[k][:, :], wrow[i // QP][:, i % QP, :],
                                        ALU.mult).then_inc(s_h, 1)
                    else:
                        ready(dve, s_lo, g - 1)
                        V.tensor_tensor(hid[k][:, :], sg[k][:, :], U_ps[k][:, :], ALU.mult).then_inc(s_h, 1)
                    for s in after:
                        s(b + 1, 1 - p, other)

            def split_lo(c, k):
                a, z = quarter(c)
                dve.wait_ge(s_whi, 3 * c + k + 1)
                dst, src, h = ((wg_lo, wg_raw, wg_hi), (wu_lo, wu_raw, wu_hi), (wd_lo, wd_raw, wd_hi))[k]
                V.tensor_tensor(dst[:, a:z], src[:, a:z], h[:, a:z].bitcast(fp32), ALU.subtract).then_inc(s_wlo, 1)

            def prologue(*stages):
                for s in stages:
                    s(0, 0, 0)

            prologue(stats_a)
            dve.wait_ge(s_cst, 32)
            prologue(stats_b)
            V.tensor_scalar(negm_b[:, :].rearrange("p (t l) -> p t l", t=NC_),
                            bc(strict.unsqueeze(1), [128, NC_, 128]), NEG, None, ALU.mult).then_inc(s_setup_d, 1)
            V.tensor_scalar(d_ident[:, :], ident, par_sb[:, P_D:P_D + 1], None, ALU.mult).then_inc(s_setup_d, 1)
            V.memset(ones_r[:, :], 1.0).then_inc(s_setup_d, 1)
            prologue(normalise)
            dve.wait_ge(s_wshi, 1)
            V.tensor_tensor(ws_lo[:, :], ws_raw[:, :], ws_hi[:, :].bitcast(fp32), ALU.subtract).then_inc(s_wslo, 1)
            dve.wait_ge(s_setup_a, 1)
            V.tensor_scalar(neg_a[:, :], exp_a[:, :], -1.0, None, ALU.mult).then_inc(s_setup_d, 1)
            dve.wait_ge(s_setup_d, 4)
            prologue(xT_low, score_a, softplus, score_b, group_a, rank_a, rank_b, rank_c, top_a, top_b, top_c,
                     ties_a, ties_b, weights_a, weights_b)
            split_lo(0, 0)
            split_lo(0, 1)
            prologue(mask_scores, states_a, states_b)
            split_lo(0, 2)
            assert count[0] == SIDE, count[0]
            period(0, 0, 0, first=True)
            with dve.Fori(0, (NBLK - 2) // 2) as j:
                period(2 * j + 1, 1, j)
                period(2 * j + 2, 0, j + 1)
            period(NBLK - 1, 1, NBLK // 2 - 1, last=True)

        @block.gpsimd
        def _(pool):
            P = nc.gpsimd

            def rstd_(n, p):
                ready(pool, s_stats, NC_ * (n + 1))
                ready(pool, s_xn, NC_ * n)
                P.tensor_tensor(var_eps[:, :], mv[:, :, 1], eps[:, :], ALU.add).then_inc(s_pool, 1)
                ready(pool, s_pool, 2 * n + 1)
                P.tensor_tensor(rstd[:, :], var_eps[:, :], halfpow[:, :], ALU.pow).then_inc(s_rstd, 1)

            def mask_dA(n, p):
                ready(pool, s_dA, n + 1)
                P.tensor_tensor(mk[:, :, :], bc(strict.unsqueeze(1), [128, NC_, 128]),
                                bc(dA[:, :].unsqueeze(2), [128, NC_, 128]), ALU.mult).then_inc(s_mk, 1)

            def scale_BC(n, p):
                ready(pool, s_dec, n + 1)
                P.tensor_tensor(dsdt[:, :], dec[:, 0:NC_], dt_s[:, :], ALU.mult).then_inc(s_pool, 1)
                ready(pool, s_pool, 2 * n + 2)
                ready(pool, s_btok, n + 1)
                P.tensor_tensor(Bs[:, :, :], B_tok[:, 0:NC_ - 1, :], bc(dsdt[:, 0:NC_ - 1].unsqueeze(2), [128, NC_ - 1, NS]),
                                ALU.mult).then_inc(s_Bs, 1)
                ready(pool, s_ecum, n + 1)
                ready(pool, s_ct, n + 1)
                P.tensor_tensor(CTs[:, :], CT[:, C:T], ecum[:, :], ALU.mult).then_inc(s_CTs, 1)

            def add_D(n, p):
                ready(pool, s_G0, NC_ * (n + 1))
                P.tensor_tensor(G[:, :, :], G0[:, :, :], bc(d_ident[:, :].unsqueeze(1), [128, NC_, 128]),
                                ALU.add).then_inc(s_G, 1)

            side = {0: rstd_, 7: mask_dA, 10: scale_BC, 13: add_D}

            def final(b, p, half):
                ready(pool, s_go, b + 1)
                ready(pool, s_yT, b + 1)
                ready(pool, s_xf[p], 16 * (half + 1))
                P.tensor_tensor(oT[p][:, :], yT[p][:, :], gate_o[:, :], ALU.mult).then_inc(s_yg, 1)
                ready(pool, s_yg, b + 1)
                P.tensor_tensor(oT[p][:, :], oT[p][:, :], xf[p][:, :], ALU.add).then_inc(s_fin, 1)

            def lo(b, i, p):
                g = U * b + i
                ready(pool, s_hi, g + 1)
                P.tensor_tensor(h_lo[slot(i)][:, :], hid[(p + i) % 2][:, :], h_hi[slot(i)][:, :].bitcast(fp32),
                                ALU.subtract).then_inc(s_lo, 1)

            def period(b, p, half, first=False, last=False):
                for i in range(U):
                    if i == LAG + 1 and not first:
                        final(b - 1, 1 - p, half - (1 if p == 0 else 0))
                    if i in side and not last:
                        side[i](b + 1, 1 - p)
                    lo(b, i, p)

            P.memset(halfpow[:, :], -0.5).then_inc(s_setup_p, 1)
            P.memset(eps[:, :], LN_EPS).then_inc(s_setup_p, 1)
            pool.wait_ge(s_setup_p, 2)
            rstd_(0, 0)
            pool.wait_ge(s_cst, 32)
            pool.wait_ge(s_setup_d, 4)
            for i in sorted(side)[1:]:
                side[i](0, 0)
            period(0, 0, 0, first=True)
            with pool.Fori(0, (NBLK - 2) // 2) as j:
                period(2 * j + 1, 1, j)
                period(2 * j + 2, 0, j + 1)
            period(NBLK - 1, 1, NBLK // 2 - 1, last=True)
            final(NBLK - 1, 1, NBLK // 2 - 1)


def _shape_constants(np):
    k = np.arange(128)
    c = np.zeros((128, K_END), np.float32)
    c[:, K_ID:K_ID + 128] = k[:, None] == k[None, :]
    c[:, K_TRI:K_TRI + 128] = k[:, None] <= k[None, :]
    c[:, K_STRICT:K_STRICT + 128] = k[:, None] > k[None, :]
    g = np.arange(NG)
    c[:, K_BEATS:K_BEATS + NC_ * NG * NG] = np.tile((g[None, :] < g[:, None]).reshape(-1), NC_)
    c[:, K_RESET:K_RESET + NC_ * E] = np.arange(NC_ * E) % E != 0
    return c


def kernel(**inputs):
    import numpy as np
    import concourse.bacc as bacc
    from concourse import mybir as mb
    from concourse.bass_utils import run_bass_kernel_spmd as run

    a = {k: np.asarray(v) for k, v in inputs.items()}
    x = a["L0_attn_x"]
    wx = a["L0_attn_W_xproj"]
    feat = lambda w: w.reshape(-1, H).T
    pairs = np.arange(E).reshape(2, PAIRS).T.reshape(-1)
    gate = np.concatenate([feat(a["L0_ffn_gate_w"][pairs]), feat(a["L0_ffn_shared_gate_w"])], 1)
    up = np.concatenate([feat(a["L0_ffn_up_w"][pairs]), feat(a["L0_ffn_shared_up_w"])], 1)
    down = np.concatenate([a["L0_ffn_down_w"][pairs].transpose(0, 2, 1).reshape(E * I, H),
                           a["L0_ffn_shared_down_w"].T], 0)
    down = down.reshape(U, 128, H).transpose(1, 0, 2).reshape(128, U * H)
    small = np.concatenate([a["L0_ffn_router_weight"], wx[1:1 + NS], wx[0:1], wx[0:1], wx[1:]], 0).T
    row = np.concatenate([a["L0_ffn_router_bias"], a["L0_attn_dt_bias"], a["L0_attn_A_log"], a["L0_attn_D"]])
    arrays = {
        "x_tok": x.reshape(NBLK, NC_, C, H).transpose(0, 2, 1, 3),
        "x_feat": x.transpose(0, 2, 1),
        "w_gate": gate, "w_up": up, "w_down": down, "w_small": small,
        "consts": _shape_constants(np),
        "params": np.broadcast_to(row, (128, P_END)),
    }
    arrays = {k: np.ascontiguousarray(v) for k, v in arrays.items()}
    nc = bacc.Bacc("TRN2", target_bir_lowering=False, num_devices=1)
    args = [nc.dram_tensor(k, v.shape, mb.dt.from_np(v.dtype), kind="ExternalInput").ap() for k, v in arrays.items()]
    args.append(nc.dram_tensor("w_dram", (2, E, T), mb.dt.float32, kind="Internal").ap())
    out = nc.dram_tensor("out", (NBLK, H, T), mb.dt.float32, kind="ExternalOutput").ap()
    gated_ssd_moe(nc, *args, out)
    r = run(nc, [arrays], core_ids=[0])
    return np.ascontiguousarray(np.asarray(r.results[0]["out"]).transpose(0, 2, 1))
```

```python
import concourse.bass as bass
from concourse import mybir
from contextlib import ExitStack

NBLK, T, H = 8, 512, 128
C = 128
NC_ = T // C
E, I = 32, 64
PAIRS = E // 2
QUARTERS, QP = 4, PAIRS // 4
U = PAIRS + 1
NS = 64
NG, GE = 4, E // 4
TOPG, TOPK = 2, 4
SCALE = 2.5
LN_EPS = 1e-5
W_EPS = 1e-20
NEG = -30000.0
WT = 98
COL_B, COL_DT = E, E + NS
EARLY = 3
LAG = 3
TAIL = 2
HB = 4

EXP_LN_SET = 6

K_ID, K_TRI, K_STRICT, K_BEATS, K_RESET, K_PICK, K_END = 0, 128, 256, 384, 448, 576, 1088
P_BIAS, P_DTB, P_ALOG, P_D, P_END = 0, E, E + 1, E + 2, E + 3


def gated_ssd_moe(nc, x_tok, x_feat, w_gate, w_up, w_down, w_small, consts, params, w_dram, out):
    fp32, f32r, bf16 = mybir.dt.float32, mybir.dt.float32r, mybir.dt.bfloat16
    ALU = mybir.AluOpType
    ACT = mybir.ActivationFunctionType
    AXX = mybir.AxisListType.X
    ctx = ExitStack()
    with ctx:
        def sb(name, shape, dt=fp32):
            return ctx.enter_context(nc.sbuf_tensor(name, shape, dt))

        def sem(name):
            return ctx.enter_context(nc.semaphore(name))

        wg_raw, wu_raw, wd_raw = (sb(n, [128, U * 128]) for n in ("wg_raw", "wu_raw", "wd_raw"))
        wg_hi, wu_hi, wd_hi = (sb(n, [128, U * 128], f32r) for n in ("wg_hi", "wu_hi", "wd_hi"))
        wg_lo, wu_lo, wd_lo = (sb(n, [128, U * 128], f32r) for n in ("wg_lo", "wu_lo", "wd_lo"))
        ws_raw = sb("ws_raw", [128, WT + 128])
        ws_hi = sb("ws_hi", [128, WT + 128], f32r)
        ws_lo = sb("ws_lo", [128, WT + 128], f32r)
        cst = sb("cst", [128, K_END])
        par_sb = sb("par_sb", [128, P_END])
        ones_r = sb("ones_r", [128, NS], f32r)
        strict_r = sb("strict_r", [128, 128], f32r)
        halfpow = sb("halfpow", [128, NC_])
        eps = sb("eps", [128, NC_])
        ident_b = sb("ident_b", [128, 128], bf16)
        negm_b = sb("negm_b", [128, NC_ * 128], bf16)
        d_ident = sb("d_ident", [128, 128])
        neg_a = sb("neg_a", [128, 1])
        exp_a = sb("exp_a", [128, 1])
        ident = cst[:, K_ID:K_ID + 128]
        tri = cst[:, K_TRI:K_TRI + 128]
        strict = cst[:, K_STRICT:K_STRICT + 128]
        beats_lm = cst[:, K_BEATS:K_BEATS + NC_ * NG * NG]
        pick = cst[0:E, K_PICK:K_PICK + QP * 128]
        reset = cst[:, K_RESET:K_RESET + NC_ * E]

        xin = [sb(f"xin{k}", [128, NC_, H]) for k in range(2)]
        xf = [sb(f"xf{k}", [128, T]) for k in range(2)]
        xT_hi = [sb(f"xT_hi{k}", [128, T], f32r) for k in range(2)]
        xT_lo = [sb(f"xT_lo{k}", [128, T], f32r) for k in range(2)]
        wT = sb("wT", [E, T])
        wrow = [sb(f"wrow{q}", [128, QP, T]) for q in range(QUARTERS)]
        yT = [sb(f"yT{k}", [128, T]) for k in range(2)]
        oT = [sb(f"oT{k}", [128, T]) for k in range(2)]
        stats = sb("stats", [128, NC_, 6])
        mv = sb("mv", [128, NC_, 2])
        var_eps = sb("var_eps", [128, NC_])
        rstd = sb("rstd", [128, NC_])
        z_pos = sb("z_pos", [128, NC_])
        z_abs = sb("z_abs", [128, NC_])
        sp_e = sb("sp_e", [128, NC_])
        sp_l = sb("sp_l", [128, NC_])
        dt_s = sb("dt_s", [128, NC_])
        dA_hi = sb("dA_hi", [128, NC_], f32r)
        dA_lo = sb("dA_lo", [128, NC_], f32r)
        mk_hi = sb("mk_hi", [128, NC_, 128], f32r)
        mk_lo = sb("mk_lo", [128, NC_, 128], f32r)
        Lt = sb("Lt", [128, NC_, 128])
        ecum = sb("ecum", [64, 3 * 128])
        B_tok = sb("B_tok", [128, NC_, NS])
        Bs = sb("Bs", [128, 3, NS])
        BT = sb("BT", [64, T])
        CT = sb("CT", [64, T])
        CTs = sb("CTs", [64, 3 * 128])
        G = sb("G", [128, NC_, 128])
        St = [sb(f"St{k}", [64, H]) for k in range(3)]
        e_r = sb("e_r", [128, NC_, E])
        r_p1 = sb("r_p1", [128, NC_, E])
        score = sb("score", [128, NC_, E])
        sfc = sb("sfc", [128, NC_ * NG, GE + GE // 2])
        pair_sum = sb("pair_sum", [128, NC_ * NG, GE // 2 * GE])
        gsum = sb("gsum", [128, NC_, NG])
        gt_ij, ge_ij, gw_ij, bt_ij = (sb(f"{n}_ij", [128, NC_ * NG, NG]) for n in ("gt", "ge", "gw", "bt"))
        grank = sb("grank", [128, NC_ * NG])
        cand = sb("cand", [128, NC_ * NG, GE])
        top8 = sb("top8", [128, NC_, 8])
        above = sb("above", [128, NC_, E])
        equal = sb("equal", [128, NC_, E])
        n_above = sb("n_above", [128, NC_])
        room = sb("room", [128, NC_])
        nth = sb("nth", [128, NC_ * E])
        fits = sb("fits", [128, NC_, E])
        tied = sb("tied", [128, NC_, E])
        chosen = sb("chosen", [128, NC_, E])
        w0 = sb("w0", [128, NC_, E])
        wsum = sb("wsum", [128, NC_])
        wsum_e = sb("wsum_e", [128, NC_])
        wrec = sb("wrec", [128, NC_])
        wfull = sb("wfull", [128, NC_, E])
        sg = [sb(f"sg{k}", [128, T]) for k in range(2)]
        tt = [sb(f"tt{k}", [128, T]) for k in range(2)]
        hid = [sb(f"hid{k}", [128, T]) for k in range(2)]
        h_hi = [sb(f"h_hi{k}", [128, T], f32r) for k in range(HB + 1)]
        h_lo = [sb(f"h_lo{k}", [128, T], f32r) for k in range(HB + 1)]
        gate_o = sb("gate_o", [128, T])

        def bank(name):
            return ctx.enter_context(nc.psum_tensor(name, [128, T], fp32))
        G_ps = [bank("G0_ps"), bank("G1_ps")]
        U_ps = [bank("U0_ps"), bank("U1_ps")]
        O_ps, SA, SB, SC = bank("O_ps"), bank("SA"), bank("SB"), bank("SC")
        SAc, SBc, SCc = (x[:, :].rearrange("p (t c) -> p t c", t=NC_) for x in (SA, SB, SC))

        s_cst = sem("s_cst")
        s_cpick = sem("s_cpick")
        s_wsm = sem("s_wsm")
        s_w = [sem(f"s_w{c}") for c in range(4)]
        s_xin = [sem(f"s_xin{k}") for k in range(2)]
        s_xf = [sem(f"s_xf{k}") for k in range(2)]
        s_setup_p = sem("s_setup_p")
        s_setup_a = sem("s_setup_a")
        s_setup_d = sem("s_setup_d")
        s_wshi = sem("s_wshi")
        s_wslo = sem("s_wslo")
        s_whi = sem("s_whi")
        s_wlo = [sem(f"s_wlo{c}") for c in range(4)]
        s_dve = sem("s_dve")
        s_var = sem("s_var")
        s_top = sem("s_top")
        s_bn = sem("s_bn")
        s_stats = sem("s_stats")
        s_rstd = sem("s_rstd")
        s_xn = sem("s_xn")
        s_xnT_ps = sem("s_xnT_ps")
        s_xThi = sem("s_xThi")
        s_xTlo = sem("s_xTlo")
        s_ptok = sem("s_ptok")
        s_pbc = sem("s_pbc")
        s_zabs = sem("s_zabs")
        s_spe = sem("s_spe")
        s_spl = sem("s_spl")
        s_er = sem("s_er")
        s_btok = sem("s_btok")
        s_bt = sem("s_bt")
        s_ct = sem("s_ct")
        s_dA = sem("s_dA")
        s_mk = sem("s_mk")
        s_ecum_ps = sem("s_ecum_ps")
        s_seg_ps = sem("s_seg_ps")
        s_L = sem("s_L")
        s_Ldt = sem("s_Ldt")
        s_pair = sem("s_pair")
        s_sfc = sem("s_sfc")
        s_ecum = sem("s_ecum")
        s_Bs = sem("s_Bs")
        s_CTs = sem("s_CTs")
        s_sc_ps = sem("s_sc_ps")
        s_st_ps = sem("s_st_ps")
        s_G0 = sem("s_G0")
        s_G = sem("s_G")
        s_S = sem("s_S")
        s_y_ps = sem("s_y_ps")
        s_yT = sem("s_yT")
        s_w_tok = sem("s_w_tok")
        s_wT_ps = sem("s_wT_ps")
        s_wT = sem("s_wT")
        s_gate = sem("s_gate")
        s_up = sem("s_up")
        s_wdram = [sem(f"s_wdram{k}") for k in range(2)]
        s_pick = sem("s_pick")
        s_picked = sem("s_picked")
        s_wrow = [sem(f"s_wrow{q}") for q in range(QUARTERS)]
        s_silu = sem("s_silu")
        s_t = sem("s_t")
        s_h = sem("s_h")
        s_hi = sem("s_hi")
        s_lo = sem("s_lo")
        s_down = sem("s_down")
        s_go = sem("s_go")
        s_yg = sem("s_yg")
        s_fin = sem("s_fin")
        s_held = sem("s_held")
        s_out = [sem(f"s_out{k}") for k in range(2)]

        def ready(eng, semaphore, value):
            if isinstance(value, int) and value <= 0:
                return
            eng.wait_ge(semaphore, value)

        def hold(eng, semaphore, value):
            eng.wait_ge(semaphore, value)
            eng.sem_inc(s_held, 1)

        def read_two_ago(eng, b, i):
            if i == 1:
                ready(eng, s_h, U * b)
            else:
                ready(eng, s_t, PAIRS * b + (i - 1 if i else 0))

        def bc(ap, shape):
            return ap.to_broadcast(shape)

        def slot(i):
            return i % HB if i < PAIRS else HB

        def quarter(c):
            return c * 4 * 128, (c + 1) * 4 * 128 if c < 3 else U * 128

        def split_lo(wait, engine, c, ks=range(3)):
            a, z = quarter(c)
            for k in ks:
                dst, src, h = ((wg_lo, wg_raw, wg_hi), (wu_lo, wu_raw, wu_hi), (wd_lo, wd_raw, wd_hi))[k]
                wait.wait_ge(s_whi, 3 * c + k + 1)
                engine.tensor_tensor(dst[:, a:z], src[:, a:z], h[:, a:z].bitcast(fp32),
                                     ALU.subtract).then_inc(s_wlo[c], 1)

        def pair_sums(wait, engine, n):
            ready(wait, s_sfc, 2 * (n + 1))
            near = bc(sfc[:, :, 0:GE].unsqueeze(2), [128, NC_ * NG, GE // 2, GE])
            far = bc(sfc[:, :, 1:1 + GE].unsqueeze(2), [128, NC_ * NG, GE // 2, GE])
            ap = [list(x) for x in far.ap]
            ap[2][0] = 1
            far = bass.AP(tensor=far.tensor, offset=far.offset, ap=ap)
            engine.tensor_tensor(pair_sum[:, :, :].rearrange("p a (d e) -> p a d e", e=GE), near, far,
                                 ALU.add).then_inc(s_pair, 1)

        def lo(wait, engine, b, i, p):
            ready(wait, s_hi, U * b + i + 1)
            engine.tensor_tensor(h_lo[slot(i)][:, :], hid[(p + i) % 2][:, :], h_hi[slot(i)][:, :].bitcast(fp32),
                                 ALU.subtract).then_inc(s_lo, 1)

        def final(wait, engine, b, p, half):
            ready(wait, s_go, b + 1)
            ready(wait, s_yT, b + 1)
            ready(wait, s_xf[p], 16 * (half + 1))
            engine.tensor_tensor(oT[p][:, :], yT[p][:, :], gate_o[:, :], ALU.mult).then_inc(s_yg, 1)
            ready(wait, s_yg, b + 1)
            engine.tensor_tensor(oT[p][:, :], oT[p][:, :], xf[p][:, :], ALU.add).then_inc(s_fin, 1)

        block = ctx.enter_context(nc.Block())

        def store(sp, b):
            ready(sp, s_fin, b + 1)
            sp.dma_start(out[b], oT[b % 2][:, :]).then_inc(s_out[b % 2], 16)
            if b + 2 < NBLK:
                sp.wait_ge(s_out[b % 2], 16 * (b // 2 + 1))
                sp.dma_start(xf[b % 2][:, :], x_feat[b + 2]).then_inc(s_xf[b % 2], 16)

        @block.sync
        def _(sp):
            def spread_weights(n):
                k = n % 2
                ready(sp, s_wT, n + 1)
                sp.dma_start(w_dram[k], wT[:, :]).then_inc(s_wdram[k], 16)
                sp.wait_ge(s_wdram[k], 16 * (n // 2 + 1))
                for q in range(QUARTERS):
                    if q == QUARTERS - 1 and n + 1 < NBLK:
                        ready(sp, s_y_ps, n + 1)
                        sp.dma_start(xin[k][:, :, :], x_tok[min(n + 2, NBLK - 1)]).then_inc(s_xin[k], 16)
                    if n == 0 and q == 0:
                        continue
                    ready(sp, s_h, U * (n - 1) + (q + 1) * QP)
                    for half in range(2):
                        e0 = half * PAIRS + q * QP
                        rows = w_dram[k, e0:e0 + QP, :].rearrange("e t -> (e t)").unsqueeze(0)
                        sp.dma_start(wrow[q][half * I:(half + 1) * I, :, :].rearrange("p e t -> p (e t)"),
                                     rows.to_broadcast([I, QP * T])).then_inc(s_wrow[q], 16)

            sp.dma_start(xin[0][:, :, :], x_tok[0]).then_inc(s_xin[0], 16)
            sp.dma_start(cst[:, 0:K_PICK], consts[:, 0:K_PICK]).then_inc(s_cst, 16)
            sp.dma_start(par_sb[:, :], params[:, :]).then_inc(s_cst, 16)
            sp.dma_start(ws_raw[:, :], w_small[:, :]).then_inc(s_wsm, 16)
            for c in range(4):
                a, z = quarter(c)
                for dst, src in ((wg_raw, w_gate), (wu_raw, w_up), (wd_raw, w_down)):
                    sp.dma_start(dst[:, a:z], src[:, a:z]).then_inc(s_w[c], 16)
                if c == 0:
                    sp.dma_start(xin[1][:, :, :], x_tok[1]).then_inc(s_xin[1], 16)
            sp.dma_start(cst[:, K_PICK:K_END], consts[:, K_PICK:K_END]).then_inc(s_cpick, 16)
            for k in range(2):
                sp.dma_start(xf[k][:, :], x_feat[k]).then_inc(s_xf[k], 16)
            spread_weights(0)
            for b in range(NBLK):
                if b > 0:
                    store(sp, b - 1)
                if b + 1 < NBLK:
                    spread_weights(b + 1)
            store(sp, NBLK - 1)
            for k in range(2):
                sp.wait_ge(s_out[k], 16 * NBLK // 2)

        @block.tensor
        def _(pe):
            mkh, mkl = (m[:, :, :].rearrange("p t l -> p (t l)") for m in (mk_hi, mk_lo))

            def three(ps, a_hi, a_lo, x_hi, x_lo):
                nc.tensor.matmul(ps, a_lo, x_hi, start=True, stop=False)
                nc.tensor.matmul(ps, a_hi, x_lo, start=False, stop=False)
                return nc.tensor.matmul(ps, a_hi, x_hi, start=False, stop=True)

            def transpose_xn(n, p):
                ready(pe, s_S, n)
                for t in range(NC_):
                    ready(pe, s_xn, NC_ * n + t + 1)
                    m = nc.tensor.transpose(SAc[:, t, :], xin[p][:, t, :], ident)
                m.then_inc(s_xnT_ps, 1)

            def project(n, p):
                ready(pe, s_xTlo, n + 1)
                ready(pe, s_yT, n)
                for t in range(NC_):
                    c = slice(t * C, (t + 1) * C)
                    m = three(SBc[:, t, 0:WT], xT_hi[p][:, c], xT_lo[p][:, c],
                              ws_hi[:, 0:WT], ws_lo[:, 0:WT])
                m.then_inc(s_ptok, 1)
                ready(pe, s_G0, n)
                three(SC[:, :], ws_hi[:, WT:WT + 128], ws_lo[:, WT:WT + 128],
                      xT_hi[p][:, :], xT_lo[p][:, :]).then_inc(s_pbc, 1)

            def decays(n, p):
                ready(pe, s_mk, 2 * (n + 1))
                nc.tensor.matmul(SA[0:NS, C:T], ones_r[:, :], mkh[:, C:T], start=True, stop=False)
                nc.tensor.matmul(SA[0:NS, C:T], ones_r[:, :], mkl[:, C:T], start=False,
                                 stop=True).then_inc(s_ecum_ps, 1)
                ready(pe, s_btok, n + 1)
                nc.tensor.matmul(SB[:, :], strict_r[:, :], mkh, start=True, stop=False)
                nc.tensor.matmul(SB[:, :], strict_r[:, :], mkl, start=False, stop=False)
                nc.tensor.matmul(SB[:, :], ident_b[:, :], negm_b[:, :], start=False,
                                 stop=True).then_inc(s_seg_ps, 1)

            def transpose_w(n, p):
                ready(pe, s_w_tok, n + 1)
                hold(pe, s_L, n + 1)
                for t in range(NC_):
                    m = nc.tensor.transpose(SB[0:E, t * C:(t + 1) * C], wfull[:, t, :], ident)
                m.then_inc(s_wT_ps, 1)

            def scores(n, p):
                ready(pe, s_ct, n + 1)
                for t in range(NC_):
                    c = slice(t * C, (t + 1) * C)
                    m = nc.tensor.matmul(SCc[:, t, :], BT[:, c], CT[:, c], start=True, stop=True)
                m.then_inc(s_sc_ps, 1)

            def states(n, p):
                ready(pe, s_ecum, n + 1)
                ready(pe, s_Bs, n + 1)
                for t in range(NC_ - 1):
                    m = nc.tensor.matmul(SA[0:NS, t * C:(t + 1) * C], Bs[:, t, :], xin[p][:, t, :],
                                         start=True, stop=True)
                m.then_inc(s_st_ps, 1)

            def mix(n, p):
                ready(pe, s_G, n + 1)
                ready(pe, s_S, n + 1)
                ready(pe, s_CTs, n + 1)
                ready(pe, s_wT, n + 1)
                if isinstance(n, int) and n == 0:
                    pe.wait_ge(s_picked, 2)
                for t in range(NC_):
                    m = nc.tensor.matmul(SBc[:, t, :], xin[p][:, t, :], G[:, t, :], start=True, stop=t == 0)
                    if t > 0:
                        m = nc.tensor.matmul(SBc[:, t, :], St[t - 1][:, :], CTs[:, (t - 1) * C:t * C],
                                             start=False, stop=True)
                m.then_inc(s_y_ps, 1)

            side = {0: transpose_xn, 3: project, 8: decays, 10: scores, 11: states, 13: transpose_w, 16: mix}

            def down(b, i):
                g = U * b + i
                if i == 0:
                    ready(pe, s_go, b)
                ready(pe, s_lo, g + 1)
                c = slice(i * 128, (i + 1) * 128)
                s = slot(i)
                nc.tensor.matmul(O_ps[:, :], wd_lo[:, c], h_hi[s][:, :], start=i == 0, stop=False)
                nc.tensor.matmul(O_ps[:, :], wd_hi[:, c], h_lo[s][:, :], start=False, stop=False)
                nc.tensor.matmul(O_ps[:, :], wd_hi[:, c], h_hi[s][:, :], start=False,
                                 stop=i == U - 1).then_inc(s_down, 1)

            def pick_pair(i, ps):
                ready(pe, s_wT, 1)
                ready(pe, s_cpick, 16)
                ready(pe, s_picked, i - 1)
                nc.tensor.matmul(ps[:, :], pick[:, i * 128:(i + 1) * 128], wT[:, :], start=True,
                                 stop=True).then_inc(s_pick, 1)

            def gate_up(b, i, p):
                g = U * b + i
                k = (p + i) % 2
                c = slice(i * 128, (i + 1) * 128)
                ready(pe, s_silu, g - 1)
                three(G_ps[k][:, :], wg_hi[:, c], wg_lo[:, c], xT_hi[p][:, :], xT_lo[p][:, :]).then_inc(s_gate, 1)
                read_two_ago(pe, b, i)
                three(U_ps[k][:, :], wu_hi[:, c], wu_lo[:, c], xT_hi[p][:, :], xT_lo[p][:, :]).then_inc(s_up, 1)

            def period(b, p, first=False, last=False):
                for i in range(EARLY if first else 0, U):
                    if first and i % 4 == 0 and i < PAIRS:
                        pe.wait_ge(s_wlo[i // 4], 3)
                    gate_up(b, i, p)
                    if first and i == EARLY:
                        pe.wait_ge(s_picked, QP)
                    if i in side and not last:
                        side[i](b + 1, 1 - p)
                    if i >= LAG:
                        down(b, i - LAG)
                    elif not first:
                        down(b - 1, U + i - LAG)

            pe.wait_ge(s_cst, 32)
            transpose_xn(0, 0)
            pe.wait_ge(s_wshi, 1)
            pe.wait_ge(s_wslo, 1)
            project(0, 0)
            pe.wait_ge(s_wlo[0], 3)
            gate_up(0, 0, 0)
            pe.wait_ge(s_setup_d, 5)
            pe.wait_ge(s_setup_a, 2)
            decays(0, 0)
            gate_up(0, 1, 0)
            scores(0, 0)
            transpose_w(0, 0)
            states(0, 0)
            pick_pair(0, O_ps)
            pick_pair(1, SB)
            gate_up(0, 2, 0)
            pick_pair(2, O_ps)
            transpose_xn(1, 1)
            mix(0, 0)
            pick_pair(3, SC)
            period(0, 0, first=True)
            with pe.Fori(0, (NBLK - 2) // 2) as j:
                period(2 * j + 1, 1)
                period(2 * j + 2, 0)
            period(NBLK - 1, 1, last=True)
            for i in range(U - LAG, U):
                down(NBLK - 1, i)

        @block.scalar
        def _(act):
            A = nc.scalar.activation

            def xT_parts(n, p):
                ready(act, s_xnT_ps, n + 1)
                A(xT_hi[p][:, :], SA[:, :], ACT.Copy).then_inc(s_xThi, 1)

            def load_exp_ln():
                nc.scalar.add_instruction(mybir.InstLoadActFuncSet(
                    name=nc.get_next_instruction_name(), engine=mybir.EngineType.Activation,
                    act_func_set_id=EXP_LN_SET))

            def exps(n, p):
                load_exp_ln()
                ready(act, s_ptok, n + 1)
                ready(act, s_dA, 2 * n)
                ready(act, s_w_tok, n)
                A(e_r[:, :, :], SBc[:, :, 0:E], ACT.Exp, scale=-1.0).then_inc(s_er, 1)
                A(z_pos[:, :], SBc[:, :, COL_DT], ACT.Relu, bias=par_sb[:, P_DTB:P_DTB + 1]).then_inc(s_zabs, 1)
                A(z_abs[:, :], SBc[:, :, COL_DT], ACT.Abs, bias=par_sb[:, P_DTB:P_DTB + 1]).then_inc(s_zabs, 1)
                ready(act, s_zabs, 2 * (n + 1))
                A(sp_e[:, :], z_abs[:, :], ACT.Exp, scale=-1.0).then_inc(s_spe, 1)
                ready(act, s_spe, n + 1)
                A(sp_l[:, :], sp_e[:, :], ACT.Ln, bias=1.0).then_inc(s_spl, 1)

            def bc_out(n, p):
                ready(act, s_Bs, n)
                A(B_tok[:, :, :], SBc[:, :, COL_B:COL_B + NS], ACT.Copy).then_inc(s_btok, 1)
                ready(act, s_pbc, n + 1)
                A(BT[:, :], SC[0:NS, :], ACT.Copy).then_inc(s_bt, 1)
                A(CT[:, :], SC[NS:2 * NS, :], ACT.Copy).then_inc(s_ct, 1)

            def decay_exps(n, p):
                ready(act, s_ecum_ps, n + 1)
                A(ecum[:, :], SA[0:NS, C:T], ACT.Exp).then_inc(s_ecum, 1)
                ready(act, s_seg_ps, n + 1)
                A(Lt[:, :, :], SBc[:, :, :], ACT.Exp).then_inc(s_L, 1)

            def w_out(n, p):
                ready(act, s_wT_ps, n + 1)
                A(wT[:, :], SB[0:E, :], ACT.Copy).then_inc(s_wT, 1)

            def pair_out(i, ps):
                ready(act, s_pick, i + 1)
                A(wrow[0][:, i, :], ps[:, :], ACT.Copy).then_inc(s_picked, 1)

            def y_out(n, p):
                ready(act, s_y_ps, n + 1)
                A(yT[p][:, :], SB[:, :], ACT.Copy).then_inc(s_yT, 1)

            side = {0: xT_parts, 3: exps, 5: bc_out, 8: decay_exps, 14: w_out, 16: y_out}

            def hi(b, i, p):
                g = U * b + i
                ready(act, s_h, g + 1)
                ready(act, s_down, g - HB + (1 if HB <= i < PAIRS else 0) if i < PAIRS else U * b)
                A(h_hi[slot(i)][:, :], hid[(p + i) % 2][:, :], ACT.Copy).then_inc(s_hi, 1)

            def split_hi(c):
                a, z = quarter(c)
                act.wait_ge(s_w[c], 48)
                for dst, src in ((wg_hi, wg_raw), (wu_hi, wu_raw), (wd_hi, wd_raw)):
                    A(dst[:, a:z], src[:, a:z], ACT.Copy).then_inc(s_whi, 1)

            def silu(b, i, p):
                k = (p + i) % 2
                ready(act, s_gate, U * b + i + 1)
                read_two_ago(act, b, i)
                A(sg[k][:, :], G_ps[k][:, :], ACT.Silu).then_inc(s_silu, 1)

            def period(b, p, first=False, last=False):
                for i in range(U):
                    if i == LAG and not first:
                        gate_out(b - 1)
                    if i >= EARLY or not first:
                        silu(b, i, p)
                    if i > 0:
                        hi(b, i - 1, p)
                    elif not first:
                        hi(b - 1, U - 1, 1 - p)
                    if i in side and not last:
                        side[i](b + 1, 1 - p)
                    if first and i == 1:
                        y_out(0, 0)
                    if first and i < 2:
                        pair_out(2 + i, (O_ps, SC)[i])

            def gate_out(b):
                ready(act, s_down, U * (b + 1))
                A(gate_o[:, :], O_ps[:, :], ACT.Silu).then_inc(s_go, 1)

            act.wait_ge(s_cst, 32)
            A(exp_a[:, :], par_sb[:, P_ALOG:P_ALOG + 1], ACT.Exp).then_inc(s_setup_a, 1)
            A(ident_b[:, :], ident, ACT.Copy).then_inc(s_setup_a, 1)
            act.wait_ge(s_wsm, 16)
            A(ws_hi[:, :], ws_raw[:, :], ACT.Copy).then_inc(s_wshi, 1)

            xT_parts(0, 0)
            split_hi(0)
            exps(0, 0)
            bc_out(0, 0)
            for c in range(1, 4):
                split_hi(c)
            decay_exps(0, 0)
            silu(0, 0, 0)
            w_out(0, 0)
            silu(0, 1, 0)
            pair_out(0, O_ps)
            pair_out(1, SB)
            silu(0, 2, 0)
            period(0, 0, first=True)
            with act.Fori(0, (NBLK - 2) // 2) as j:
                period(2 * j + 1, 1)
                period(2 * j + 2, 0)
            period(NBLK - 1, 1, last=True)
            hi(NBLK - 1, U - 1, 1)
            gate_out(NBLK - 1)

        @block.vector
        def _(dve):
            V = nc.vector
            SIDE = 24
            count = [0]

            def step(n, make, *args, wait=True, **kw):
                if wait:
                    ready(dve, s_dve, SIDE * n + count[0])
                count[0] += 1
                return make(*args, **kw).then_inc(s_dve, 1)

            def stats_a(n, p, half):
                ready(dve, s_xin[p], 16 * (half + 1))
                ready(dve, s_rstd, n)
                for t in range(NC_):
                    V.bn_stats(stats[:, t, :], xin[p][:, t, :]).then_inc(s_bn, 1)

            def stats_b(n, p, half):
                hold(dve, s_bn, NC_ * (n + 1))
                for t in range(NC_):
                    V.bn_aggr(mv[:, t, :], stats[:, t, :]).then_inc(s_stats, 1)

            def normalise(n, p, half):
                ready(dve, s_rstd, n + 1)
                for t in range(NC_):
                    V.tensor_scalar(xin[p][:, t, :], xin[p][:, t, :], mv[:, t, 0:1], rstd[:, t:t + 1],
                                    ALU.subtract, ALU.mult).then_inc(s_xn, 1)

            def xT_low(n, p, half):
                ready(dve, s_xThi, n + 1)
                V.tensor_tensor(xT_lo[p][:, :], SA[:, :], xT_hi[p][:, :].bitcast(fp32),
                                ALU.subtract).then_inc(s_xTlo, 1)

            def one_plus(n, p, half):
                count[0] = 0
                ready(dve, s_er, n + 1)
                step(n, V.tensor_scalar, r_p1[:, :, :], e_r[:, :, :], 1.0, None, ALU.add, wait=False)

            def softplus(n, p, half):
                ready(dve, s_spl, n + 1)
                step(n, V.tensor_tensor, dt_s[:, :], z_pos[:, :], sp_l[:, :], ALU.add, wait=False)
                ready(dve, s_dve, SIDE * n + count[0])
                V.tensor_scalar(dA_hi[:, :], dt_s[:, :], neg_a[:, 0:1], None, ALU.mult).then_inc(s_dA, 1)
                ready(dve, s_dA, 2 * n + 1)
                V.scalar_tensor_tensor(dA_lo[:, :], dt_s[:, :], neg_a[:, 0:1], dA_hi[:, :].bitcast(fp32), ALU.mult,
                                       ALU.subtract).then_inc(s_dA, 1)

            def score_a(n, p, half):
                step(n, V.reciprocal, score[:, :, :], r_p1[:, :, :])

            def score_b(n, p, half):
                s16 = score[:, :, :].rearrange("p t (g e) -> p t g e", g=NG)
                b16 = par_sb[:, P_BIAS:P_BIAS + E].rearrange("p (g e) -> p g e", g=NG)
                sf = sfc[:, :, :].rearrange("p (t g) e -> p t g e", g=NG)
                bb = bc(b16.unsqueeze(1), [128, NC_, NG, GE])
                ready(dve, s_dve, SIDE * n + count[0])
                V.tensor_tensor(sf[:, :, :, 0:GE], s16, bb, ALU.add).then_inc(s_sfc, 1)
                V.tensor_tensor(sf[:, :, :, GE:GE + GE // 2], s16[:, :, :, 0:GE // 2],
                                bb[:, :, :, 0:GE // 2], ALU.add).then_inc(s_sfc, 1)

            def group_a(n, p, half):
                ready(dve, s_pair, n + 1)
                step(n, V.tensor_reduce, gsum[:, :, :].rearrange("p t g -> p (t g)"), pair_sum[:, :, :],
                     axis=AXX, op=ALU.max, wait=False)

            def rank_a(n, p, half):
                gj = bc(gsum[:, :, :].unsqueeze(2), [128, NC_, NG, NG])
                gi = bc(gsum[:, :, :].unsqueeze(3), [128, NC_, NG, NG])
                v4 = lambda t_: t_[:, :, :].rearrange("p (t i) j -> p t i j", i=NG)
                step(n, V.tensor_tensor, v4(ge_ij), gj, gi, ALU.is_ge)
                step(n, V.tensor_tensor, v4(gt_ij), gj, gi, ALU.is_gt, wait=False)

            def rank_b(n, p, half):
                flat = lambda t_: t_[:, :, :].rearrange("p a j -> p (a j)")
                step(n, V.tensor_tensor, flat(gw_ij), flat(ge_ij), beats_lm, ALU.mult)
                step(n, V.tensor_tensor, flat(bt_ij), flat(gw_ij), flat(gt_ij), ALU.max)

            def rank_c(n, p, half):
                step(n, V.tensor_reduce, grank[:, :], bt_ij[:, :, :], axis=AXX, op=ALU.add)
                step(n, V.scalar_tensor_tensor, cand[:, :, :], bc(grank[:, :].unsqueeze(2), [128, NC_ * NG, GE]),
                     TOPG - 0.5, sfc[:, :, 0:GE], ALU.is_lt, ALU.mult)

            c4 = cand[:, :, :].rearrange("p (t g) e -> p t (g e)", g=NG)

            def top_a(n, p, half):
                hold(dve, s_dve, SIDE * n + count[0])
                for t in range(NC_):
                    V.max(top8[:, t, :], c4[:, t, :]).then_inc(s_top, 1)

            def top_b(n, p, half):
                kth = bc(top8[:, :, TOPK - 1:TOPK], [128, NC_, E])
                ready(dve, s_top, NC_ * (n + 1))
                step(n, V.tensor_tensor, above[:, :, :], c4, kth, ALU.is_gt, wait=False)
                step(n, V.tensor_tensor, equal[:, :, :], c4, kth, ALU.is_equal, wait=False)

            def top_c(n, p, half):
                step(n, V.tensor_reduce, n_above[:, :], above[:, :, :], axis=AXX, op=ALU.add)
                step(n, V.tensor_tensor_scan, nth[:, :], reset, equal[:, :, :].rearrange("p t e -> p (t e)"), 0.0,
                     ALU.mult, ALU.add, wait=False)
                ready(dve, s_dve, SIDE * n + count[0] - 1)
                step(n, V.tensor_scalar, room[:, :], n_above[:, :], -1.0, float(TOPK), ALU.mult, ALU.add, wait=False)

            def ties_a(n, p, half):
                step(n, V.tensor_tensor, fits[:, :, :], nth[:, :].rearrange("p (t e) -> p t e", e=E),
                     bc(room[:, :].unsqueeze(2), [128, NC_, E]), ALU.is_le)
                step(n, V.tensor_tensor, tied[:, :, :], fits[:, :, :], equal[:, :, :], ALU.mult)

            def ties_b(n, p, half):
                step(n, V.tensor_tensor, chosen[:, :, :], tied[:, :, :], above[:, :, :], ALU.add)
                step(n, V.tensor_tensor, w0[:, :, :], chosen[:, :, :], score[:, :, :], ALU.mult)

            def weights_a(n, p, half):
                step(n, V.tensor_reduce, wsum[:, :], w0[:, :, :], axis=AXX, op=ALU.add)
                step(n, V.tensor_scalar, wsum_e[:, :], wsum[:, :], W_EPS, None, ALU.add)

            def weights_b(n, p, half):
                step(n, V.reciprocal, wrec[:, :], wsum_e[:, :])
                ready(dve, s_dve, SIDE * n + count[0])
                V.scalar_tensor_tensor(wfull[:, :, :], w0[:, :, :], SCALE, bc(wrec[:, :].unsqueeze(2), [128, NC_, E]),
                                       ALU.mult, ALU.mult).then_inc(s_w_tok, 1)

            def mask_scores(n, p, half):
                ready(dve, s_sc_ps, n + 1)
                ready(dve, s_Ldt, n + 1)
                ready(dve, s_y_ps, n)
                V.tensor_tensor(G[:, :, :], SCc[:, :, :], Lt[:, :, :], ALU.mult).then_inc(s_G0, 1)

            def states_a(n, p, half):
                ready(dve, s_st_ps, n + 1)
                ready(dve, s_ecum, n + 1)
                step(n, V.tensor_copy, St[0][:, :], SA[0:NS, 0:C], wait=False)
                step(n, V.scalar_tensor_tensor, St[1][:, :], St[0][:, :], ecum[:, C - 1:C], SA[0:NS, C:2 * C],
                     ALU.mult, ALU.add)

            def states_b(n, p, half):
                ready(dve, s_dve, SIDE * n + count[0])
                V.scalar_tensor_tensor(St[2][:, :], St[1][:, :], ecum[:, 2 * C - 1:2 * C], SA[0:NS, 2 * C:3 * C],
                                       ALU.mult, ALU.add).then_inc(s_S, 1)

            side = {1: ([], [xT_low]), 4: ([one_plus], [softplus]), 5: ([score_a], [score_b]),
                    8: ([group_a, rank_a, rank_b, rank_c], [top_a, top_b]), 9: ([top_c], [ties_a]),
                    10: ([ties_b], [weights_a]), 11: ([weights_b], []), 12: ([mask_scores], [states_a]),
                    13: ([states_b], [])}
            norm = {3: ([], [stats_a, stats_b]), 13: ([], [normalise])}

            splits = {0: (2, 0), 1: (2, 1), 2: (2, 2), 3: (3, 0), 4: (3, 1), 8: (3, 2)}

            def gated(b, i, p):
                g = U * b + i
                k = (p + i) % 2
                ready(dve, s_silu, g + 1)
                ready(dve, s_up, g + 1)
                ready(dve, s_h, g - 1)
                V.tensor_tensor(tt[k][:, :], sg[k][:, :], U_ps[k][:, :], ALU.mult).then_inc(s_t, 1)

            def period(b, p, half, first=False, last=False):
                other = half + (1 if p == 1 else 0)
                for i in range(U):
                    g = U * b + i
                    k = (p + i) % 2
                    before, after = side.get(i, ([], [])) if not last else ([], [])
                    nbefore, nafter = norm.get(i, ([], [])) if not last else ([], [])
                    if i < PAIRS:
                        if i > 1 or not first:
                            gated(b, i, p)
                        for s in before:
                            s(b + 1, 1 - p, other)
                        for s in nbefore:
                            s(b + 2, p, half + 1)
                        if first and i < QP:
                            ready(dve, s_picked, i + 1)
                        elif i % QP == 0:
                            ready(dve, s_wrow[i // QP], 32 * (b + (1 if i else 0)))
                        ready(dve, s_t, PAIRS * b + i + 1)
                        ready(dve, s_lo, g - 1)
                        V.tensor_tensor(hid[k][:, :], tt[k][:, :], wrow[i // QP][:, i % QP, :],
                                        ALU.mult).then_inc(s_h, 1)
                    else:
                        ready(dve, s_silu, g + 1)
                        ready(dve, s_up, g + 1)
                        ready(dve, s_lo, g - 1)
                        V.tensor_tensor(hid[k][:, :], sg[k][:, :], U_ps[k][:, :], ALU.mult).then_inc(s_h, 1)
                    if last and i > U - TAIL:
                        lo(dve, V, b, i - 1, p)
                    for s in after:
                        s(b + 1, 1 - p, other)
                    if first and i in splits:
                        split_lo(dve, V, splits[i][0], splits[i][1:])
                    for s in nafter:
                        s(b + 2, p, half + 1)

            def prologue(*stages):
                for s in stages:
                    s(0, 0, 0)

            prologue(stats_a)
            dve.wait_ge(s_cst, 32)
            prologue(stats_b)
            V.tensor_scalar(negm_b[:, :].rearrange("p (t l) -> p t l", t=NC_),
                            bc(strict.unsqueeze(1), [128, NC_, 128]), NEG, None, ALU.mult).then_inc(s_setup_d, 1)
            V.tensor_scalar(d_ident[:, :], ident, par_sb[:, P_D:P_D + 1], None, ALU.mult).then_inc(s_setup_d, 1)
            V.tensor_scalar(ones_r[:, :], ident[:, 0:NS], 0.0, 1.0, ALU.mult, ALU.add).then_inc(s_setup_d, 1)
            V.tensor_copy(strict_r[:, :], strict).then_inc(s_setup_d, 1)
            prologue(normalise)
            dve.wait_ge(s_wshi, 1)
            V.tensor_tensor(ws_lo[:, :], ws_raw[:, :], ws_hi[:, :].bitcast(fp32), ALU.subtract).then_inc(s_wslo, 1)
            dve.wait_ge(s_setup_a, 1)
            V.tensor_scalar(neg_a[:, :], exp_a[:, :], -1.0, None, ALU.mult).then_inc(s_setup_d, 1)
            dve.wait_ge(s_setup_d, 5)
            xT_low(0, 0, 0)
            for stage in (stats_a, stats_b, normalise):
                stage(1, 1, 0)
            prologue(one_plus, score_a, softplus, score_b)
            pair_sums(dve, V, 0)
            prologue(group_a, rank_a, rank_b, rank_c, top_a, top_b, top_c,
                     ties_a, ties_b, weights_a, weights_b)
            gated(0, 0, 0)
            gated(0, 1, 0)
            prologue(mask_scores, states_a, states_b)
            assert count[0] == SIDE, count[0]
            period(0, 0, 0, first=True)
            with dve.Fori(0, (NBLK - 2) // 2) as j:
                period(2 * j + 1, 1, j)
                period(2 * j + 2, 0, j + 1)
            period(NBLK - 1, 1, NBLK // 2 - 1, last=True)
            lo(dve, V, NBLK - 1, U - 1, 1)
            final(dve, V, NBLK - 1, 1, NBLK // 2 - 1)

        @block.gpsimd
        def _(pool):
            P = nc.gpsimd

            def rstd_(n, p):
                ready(pool, s_stats, NC_ * (n + 1))
                ready(pool, s_xn, NC_ * n)
                P.tensor_tensor(var_eps[:, :], mv[:, :, 1], eps[:, :], ALU.add).then_inc(s_var, 1)
                ready(pool, s_var, n + 1)
                P.tensor_tensor(rstd[:, :], var_eps[:, :], halfpow[:, :], ALU.pow).then_inc(s_rstd, 1)

            def mask_dA(n, p):
                for k, (m, d) in enumerate(((mk_hi, dA_hi), (mk_lo, dA_lo))):
                    ready(pool, s_dA, 2 * n + k + 1)
                    P.tensor_tensor(m[:, :, :], bc(tri.unsqueeze(1), [128, NC_, 128]),
                                    bc(d[:, :].bitcast(fp32).unsqueeze(2), [128, NC_, 128]),
                                    ALU.mult).then_inc(s_mk, 1)

            def sum_pairs(n, p):
                pair_sums(pool, P, n)

            def scale_BC(n, p):
                ready(pool, s_Ldt, n + 1)
                ready(pool, s_btok, n + 1)
                P.tensor_tensor(Bs[:, :, :], B_tok[:, 0:NC_ - 1, :],
                                bc(Lt[:, 0:NC_ - 1, C - 1:C], [128, NC_ - 1, NS]), ALU.mult).then_inc(s_Bs, 1)
                ready(pool, s_ecum, n + 1)
                ready(pool, s_ct, n + 1)
                P.tensor_tensor(CTs[:, :], CT[:, C:T], ecum[:, :], ALU.mult).then_inc(s_CTs, 1)

            def scale_L(n, p):
                ready(pool, s_L, n + 1)
                P.tensor_tensor(Lt[:, :, :], Lt[:, :, :], bc(dt_s[:, :].unsqueeze(2), [128, NC_, 128]),
                                ALU.mult).then_inc(s_Ldt, 1)

            def add_D(n, p):
                ready(pool, s_G0, n + 1)
                P.tensor_tensor(G[:, :, :], G[:, :, :], bc(d_ident[:, :].unsqueeze(1), [128, NC_, 128]),
                                ALU.add).then_inc(s_G, 1)

            side = {5: [mask_dA], 6: [sum_pairs], 8: [scale_L, scale_BC], 13: [add_D]}

            def period(b, p, half, first=False, last=False):
                for i in range(U):
                    if i == LAG and not first:
                        final(pool, P, b - 1, 1 - p, half - (1 if p == 0 else 0))
                    if i == LAG and not last:
                        rstd_(b + 2, p)
                    for s in side.get(i, []) if not last else []:
                        s(b + 1, 1 - p)
                    if i < U - TAIL or not last:
                        lo(pool, P, b, i, p)

            P.memset(halfpow[:, :], -0.5).then_inc(s_setup_p, 1)
            P.memset(eps[:, :], LN_EPS).then_inc(s_setup_p, 1)
            pool.wait_ge(s_setup_p, 2)
            rstd_(0, 0)
            pool.wait_ge(s_cst, 32)
            pool.wait_ge(s_setup_d, 5)
            rstd_(1, 1)
            split_lo(pool, P, 0)
            mask_dA(0, 0)
            split_lo(pool, P, 1)
            for stage in (scale_L, scale_BC, add_D):
                stage(0, 0)
            period(0, 0, 0, first=True)
            with pool.Fori(0, (NBLK - 2) // 2) as j:
                period(2 * j + 1, 1, j)
                period(2 * j + 2, 0, j + 1)
            period(NBLK - 1, 1, NBLK // 2 - 1, last=True)


def _shape_constants(np):
    k = np.arange(128)
    c = np.zeros((128, K_END), np.float32)
    c[:, K_ID:K_ID + 128] = k[:, None] == k[None, :]
    c[:, K_TRI:K_TRI + 128] = k[:, None] <= k[None, :]
    c[:, K_STRICT:K_STRICT + 128] = k[:, None] > k[None, :]
    g = np.arange(NG)
    c[:, K_BEATS:K_BEATS + NC_ * NG * NG] = np.tile((g[None, :] < g[:, None]).reshape(-1), NC_)
    c[:, K_RESET:K_RESET + NC_ * E] = np.arange(NC_ * E) % E != 0
    for q in range(QP):
        for half in range(2):
            a = K_PICK + q * 128 + half * I
            c[half * PAIRS + q, a:a + I] = 1
    return c


def kernel(**inputs):
    import numpy as np
    import concourse.bacc as bacc
    from concourse import mybir as mb
    from concourse.bass_utils import run_bass_kernel_spmd as run

    a = {k: np.asarray(v) for k, v in inputs.items()}
    x = a["L0_attn_x"]
    wx = a["L0_attn_W_xproj"]
    feat = lambda w: w.reshape(-1, H).T
    pairs = np.arange(E).reshape(2, PAIRS).T.reshape(-1)
    gate = np.concatenate([feat(a["L0_ffn_gate_w"][pairs]), feat(a["L0_ffn_shared_gate_w"])], 1)
    up = np.concatenate([feat(a["L0_ffn_up_w"][pairs]), feat(a["L0_ffn_shared_up_w"])], 1)
    down = np.concatenate([a["L0_ffn_down_w"][pairs].transpose(0, 2, 1).reshape(E * I, H),
                           a["L0_ffn_shared_down_w"].T], 0)
    down = down.reshape(U, 128, H).transpose(1, 0, 2).reshape(128, U * H)
    small = np.concatenate([a["L0_ffn_router_weight"], wx[1:1 + NS], wx[0:1], wx[0:1], wx[1:]], 0).T
    row = np.concatenate([a["L0_ffn_router_bias"], a["L0_attn_dt_bias"], a["L0_attn_A_log"], a["L0_attn_D"]])
    arrays = {
        "x_tok": x.reshape(NBLK, NC_, C, H).transpose(0, 2, 1, 3),
        "x_feat": x.transpose(0, 2, 1),
        "w_gate": gate, "w_up": up, "w_down": down, "w_small": small,
        "consts": _shape_constants(np),
        "params": np.broadcast_to(row, (128, P_END)),
    }
    arrays = {k: np.ascontiguousarray(v) for k, v in arrays.items()}
    nc = bacc.Bacc("TRN2", target_bir_lowering=False, num_devices=1)
    args = [nc.dram_tensor(k, v.shape, mb.dt.from_np(v.dtype), kind="ExternalInput").ap() for k, v in arrays.items()]
    args.append(nc.dram_tensor("w_dram", (2, E, T), mb.dt.float32, kind="Internal").ap())
    out = nc.dram_tensor("out", (NBLK, H, T), mb.dt.float32, kind="ExternalOutput").ap()
    gated_ssd_moe(nc, *args, out)
    r = run(nc, [arrays], core_ids=[0])
    return np.ascontiguousarray(np.asarray(r.results[0]["out"]).transpose(0, 2, 1))
```
